# Optimizing a Trainium2 kernel written in Bass

```python
import numpy as np
import jax
import jax.numpy as jnp

def _softmax(x, axis=-1):
    return jax.nn.softmax(x, axis=axis)

def _gelu(x):
    return jax.nn.gelu(x, approximate=True)

def _silu(x):
    return jax.nn.silu(x)

def _sigmoid(x):
    return jax.nn.sigmoid(x)

def _layernorm(x, axis=-1, eps=1e-05):
    m = jnp.mean(x, axis=axis, keepdims=True)
    v = jnp.var(x, axis=axis, keepdims=True)
    return (x - m) / jnp.sqrt(v + eps)

def _scatter_add(tgt, idx, src, axis=0):
    return tgt.at[idx].add(src)

def _segment_sum(src, seg, n):
    return jax.ops.segment_sum(src, seg, n)
kernel_name = 'mk_prb_d1_jaxref_r8_7a434a'

def setup_inputs(seed: int=0):
    np.random.seed(seed)
    _w = jnp.asarray

    def _L0_attn_setup():
        import jax, jax.numpy as jnp
        import numpy as np
        B, N, D = (8, 128, 512)
        H = 8
        HEAD_DIM = D // H
        E = HEAD_DIM // H
        key = jax.random.key(seed)
        ks = jax.random.split(key, 7)
        s = 0.02
        return {'x': jax.random.normal(ks[0], (B, N, D), dtype=jnp.float32), 'Wqk_w': jax.random.normal(ks[1], (2 * HEAD_DIM, D), dtype=jnp.float32) * s, 'Wqk_b': jnp.zeros((2 * HEAD_DIM,), dtype=jnp.float32), 'Wv_w': jax.random.normal(ks[2], (HEAD_DIM, D), dtype=jnp.float32) * s, 'Wv_b': jnp.zeros((HEAD_DIM,), dtype=jnp.float32), 'Wo_w': jax.random.normal(ks[3], (D, HEAD_DIM), dtype=jnp.float32) * s, 'Wo_b': jnp.zeros((D,), dtype=jnp.float32)}
    _L0_attn_in = _L0_attn_setup()

    def _L0_ffn_setup():
        import jax, jax.numpy as jnp
        import numpy as np
        TOP_K = 2
        key = jax.random.key(seed)
        k0, k1, k2 = jax.random.split(key, 3)
        B, S, D, H, E = (4, 256, 512, 512, 8)
        sc = 1.0 / np.sqrt(D).astype(np.float32)
        x = jax.random.normal(k0, (B, S, D), dtype=jnp.float32)
        W_gate = jax.random.normal(k1, (D, E), dtype=jnp.float32) * sc
        b_gate = jnp.zeros((E,), dtype=jnp.float32)
        W_e = jax.random.normal(k2, (E, D, H), dtype=jnp.float32) * sc
        b_e = jnp.zeros((E, H), dtype=jnp.float32)
        return {'x': x, 'W_gate': W_gate, 'b_gate': b_gate, 'W_e': W_e, 'b_e': b_e}
    _L0_ffn_in = _L0_ffn_setup()
    _d = {'L0_attn_x': _L0_attn_in['x'], 'L0_attn_Wqk_w': _L0_attn_in['Wqk_w'], 'L0_attn_Wqk_b': _L0_attn_in['Wqk_b'], 'L0_attn_Wv_w': _L0_attn_in['Wv_w'], 'L0_attn_Wv_b': _L0_attn_in['Wv_b'], 'L0_attn_Wo_w': _L0_attn_in['Wo_w'], 'L0_attn_Wo_b': _L0_attn_in['Wo_b'], 'L0_ffn_W_gate': _L0_ffn_in['W_gate'], 'L0_ffn_b_gate': _L0_ffn_in['b_gate'], 'L0_ffn_W_e': _L0_ffn_in['W_e'], 'L0_ffn_b_e': _L0_ffn_in['b_e']}
    _x0 = _d['L0_attn_x']
    _d['L0_attn_x'] = jax.random.normal(jax.random.fold_in(jax.random.key(seed), 1), (4, 512, 512), dtype=_x0.dtype)
    del _x0
    return _d

def reference(L0_attn_x, L0_attn_Wqk_w, L0_attn_Wqk_b, L0_attn_Wv_w, L0_attn_Wv_b, L0_attn_Wo_w, L0_attn_Wo_b, L0_ffn_W_gate, L0_ffn_b_gate, L0_ffn_W_e, L0_ffn_b_e):

    def _L0_attn_ref(x, Wqk_w, Wqk_b, Wv_w, Wv_b, Wo_w, Wo_b):
        import jax, jax.numpy as jnp
        import numpy as np
        B, N, D = (8, 128, 512)
        H = 8
        HEAD_DIM = D // H
        E = HEAD_DIM // H
        b, n, _ = x.shape
        qk = (x @ Wqk_w.T + Wqk_b).reshape(b, n, H, E, 2)
        q = jnp.transpose(qk[..., 0], (0, 2, 1, 3))
        k = jnp.transpose(qk[..., 1], (0, 2, 1, 3))
        v = (x @ Wv_w.T + Wv_b).reshape(b, n, H, E)
        v = jnp.transpose(v, (0, 2, 1, 3))
        scores = jnp.einsum('bhqd,bhkd->bhqk', q, k)
        attn = jax.nn.softmax(scores, axis=-1) / jnp.asarray(HEAD_DIM ** 0.5, x.dtype)
        out = jnp.einsum('bhsl,bhlv->bhsv', attn, v)
        out = jnp.transpose(out, (0, 2, 1, 3)).reshape(b, n, H * E)
        return out @ Wo_w.T + Wo_b

    def _L0_ffn_ref(x, W_gate, b_gate, W_e, b_e):
        import jax, jax.numpy as jnp
        import numpy as np
        TOP_K = 2
        logits = x @ W_gate + b_gate
        _, top_idx = jax.lax.top_k(logits, TOP_K)
        y_all = jax.nn.relu(jnp.einsum('bsd,edh->bseh', x, W_e) + b_e)
        y = jnp.take_along_axis(y_all, top_idx[..., None], axis=2)
        return y.mean(axis=2)
    x = L0_attn_x
    xn = _layernorm(x, axis=-1)
    x = x + _L0_attn_ref(xn, L0_attn_Wqk_w, L0_attn_Wqk_b, L0_attn_Wv_w, L0_attn_Wv_b, L0_attn_Wo_w, L0_attn_Wo_b) + _L0_ffn_ref(xn, L0_ffn_W_gate, L0_ffn_b_gate, L0_ffn_W_e, L0_ffn_b_e)
    return x

_drawn_inputs = setup_inputs


def setup_inputs(seed=0):
    import zlib

    import numpy as np

    out = dict(_drawn_inputs(seed))
    spreads = {'L0_attn_Wqk_b': (0.0, 0.8),
     'L0_attn_Wv_b': (0.0, 0.8),
     'L0_attn_Wo_b': (0.0, 0.1),
     'L0_ffn_b_gate': (0.0, 0.1),
     'L0_ffn_b_e': (0.0, 0.1)}
    factors = {'L0_attn_Wqk_w': 8.0, 'L0_attn_Wv_w': 8.0, 'L0_attn_Wo_w': 8.0}
    for name, (base, spread) in spreads.items():
        noise = np.random.default_rng([zlib.crc32(name.encode()), seed]).standard_normal(out[name].shape)
        drawn = base * np.exp(spread * noise) if base else spread * noise
        out[name] = jnp.asarray(drawn.astype(out[name].dtype))
    for name, factor in factors.items():
        out[name] = (out[name] * factor).astype(out[name].dtype)
    return out
```

```python
from contextlib import ExitStack

import concourse.bass as bass
from concourse import mybir

F32 = mybir.dt.float32
F32R = mybir.dt.float32r
BF16 = mybir.dt.bfloat16
I32 = mybir.dt.int32
U32 = mybir.dt.uint32
ALU = mybir.AluOpType
ACT = mybir.ActivationFunctionType
AX = mybir.AxisListType

P = 128
B, N, D = 4, 512, 512
T = B * N
NT = T // P
KC = D // P
H, HE = 8, 8
HD = H * HE
G = 2
HG = H // G
NE, F = 8, 512
PW = 3 * HD + NE
QT = N // P
NS = (2 * T + NE * (P - 1)) // P + 1
NC = 2 * NT
EPS = 1e-5
VC = HE + 1


def attention_and_experts(nc, x, wqk, bqk, wv, bv, wo, bo, wg, bg, we, be, out):
    x_rows = x.rearrange("b n d -> (b n) d")
    out_rows = out.rearrange("b n d -> (b n) d")
    xn_dram = nc.dram_tensor("xn_rows", (T, D), F32).ap()
    y_dram = nc.dram_tensor("expert_rows", (NS * P, F), F32).ap()

    ctx = ExitStack()
    with ctx:
        def sb(name, shape, dt, where=ctx):
            return where.enter_context(nc.sbuf_tensor(name, shape, dt))

        def sem(name):
            return ctx.enter_context(nc.semaphore(name))

        ident = sb("ident", [P, P], F32)
        before = sb("before", [P, P], BF16)
        ones = sb("ones", [P, P], BF16)
        ramp_i = sb("ramp_i", [P, P], I32)
        ramp = sb("ramp", [P, P], F32)
        part_i = sb("part_i", [P, 1], I32)
        part = sb("part", [P, 1], F32)
        lower = sb("lower", [P, NE, NE], F32)
        eps_t = sb("eps_t", [P, 1], F32)
        bias_p = sb("bias_p", [P, PW], F32)
        bias_o = sb("bias_o", [P, D], F32)
        wo_hi = sb("wo_hi", [P, D], F32R)
        wo_lo = sb("wo_lo", [P, D], F32R)
        proj = sb("proj", [P, NT, PW], F32)
        slots_i = sb("slots_i", [P, 2, NT], I32)
        gather_i = sb("gather_i", [P, NS], I32)
        expert_i = sb("expert_i", [P, NS], I32)
        row_in = sb("row_in", [P, 4, D], F32)
        row_mid = sb("row_mid", [P, 4, D], F32)
        t_hi = sb("t_hi", [P, 2, D], F32R)
        t_lo = sb("t_lo", [P, 2, D], F32R)

        era = ExitStack()
        w_hi = sb("w_hi", [P, NE, KC, F], F32R, era)
        w_lo = sb("w_lo", [P, NE, KC, F], F32R, era)
        sub = ExitStack()
        stage = sb("stage", [P, 2, 2, F], F32, sub)
        wp_hi = sb("wp_hi", [P, KC, PW], F32R, sub)
        wp_lo = sb("wp_lo", [P, KC, PW], F32R, sub)
        gate_w = sb("gate_w", [P, KC, NE], F32, sub)
        stats = sb("stats", [P, 2, 2, 6], F32, sub)
        mv = sb("mv", [P, NT, 2], F32, sub)
        small = sb("small", [P, 8, NT], F32, sub)
        sub.close()
        bias_e = sb("bias_e", [P, NE, F], F32, era)
        era.close()
        rout = ExitStack()
        sb("rout_gap", [P, (2 * NE * KC * F * 4 + NE * F * 4) // 4], F32, rout)
        top_v = sb("top_v", [P, NT, 8], F32, rout)
        top_i = sb("top_i", [P, NT, 8], U32, rout)
        top_f = sb("top_f", [P, NT, 8], F32, rout)
        pick = sb("pick", [P, 2, NT, NE], F32, rout)
        mask = sb("mask", [P, NT + 1, NE], BF16, rout)
        place = sb("place", [P, NT + 1, NE], F32, rout)
        tiles_gt = sb("tiles_gt", [P, NE, NT], F32, rout)
        tri = sb("tri", [P, NE, NE], F32, rout)
        ecol = sb("ecol", [P, 4, NE], F32, rout)
        te_cmp = sb("te_cmp", [P, NS, NE], F32, rout)
        te_f = sb("te_f", [P, NS], F32, rout)
        slot_p = sb("slot_p", [P, 2, NT, NE], F32, rout)
        slot_f = sb("slot_f", [P, 2, NT], F32, rout)
        slot_r = sb("slot_r", [P, 2, 2, NT], I32, rout)
        slot_q = sb("slot_q", [P, 2, NC], F32, rout)
        hot_row = sb("hot_row", [P, 2, 4, P], BF16, rout)
        hot_tile = sb("hot_tile", [P, NC, NS], BF16, rout)
        hot_val = sb("hot_val", [P, NC, 2, NS], BF16, rout)
        tok_f = sb("tok_f", [P, 2, NS], F32, rout)
        rout.close()
        att = ExitStack()
        a_q = sb("a_q", [P, QT, G * P], F32, att)
        a_k = sb("a_k", [P, QT, G * P], F32, att)
        a_m = sb("a_m", [P, QT, G * P], F32, att)
        v_ones = sb("v_ones", [P, NT, H, VC], F32, att)
        q_t = sb("q_t", [P, 2, G, N], F32R, att)
        k_t = sb("k_t", [P, 2, G, N], F32R, att)
        k_head = sb("k_head", [P, 3, H, N], F32R, att)
        q_m = sb("q_m", [P, G, N], F32R, att)
        row_max = sb("row_max", [P, 2, H, QT], F32, att)
        probs = sb("probs", [P, 2, HG, N], F32, att)
        o_sum = sb("o_sum", [P, 2, N], F32, att)
        o_inv = sb("o_inv", [P, QT, HG], F32, att)
        o_tok = sb("o_tok", [P, QT, P], F32, att)
        o_exact = sb("o_exact", [P, QT, HD], F32, att)
        o_t = sb("o_t", [P, N], F32R, att)
        acc = sb("acc", [P, 4, D], F32, att)
        y_a = sb("y_a", [P, 4, F], F32, att)
        y_b = sb("y_b", [P, 4, F], F32, att)
        res = sb("res", [P, 4, D], F32, att)
        att.close()

        ps_s = ctx.enter_context(nc.psum_tensor("ps_s", [P, 4, 512], F32))
        ps_t = ctx.enter_context(nc.psum_tensor("ps_t", [P, 2, 512], F32))
        ps_o = ctx.enter_context(nc.psum_tensor("ps_o", [P, 512], F32))
        ps_m = ctx.enter_context(nc.psum_tensor("ps_m", [P, 512], F32))

        weights_in = sem("weights_in")
        biases_in = sem("biases_in")
        consts_ready = sem("consts_ready")
        pool_step = sem("pool_step")
        dve_step = sem("dve_step")
        weights_turned = sem("weights_turned")
        weights_split = sem("weights_split")
        x_in = [sem(f"x_in{s}") for s in range(4)]
        xn_out = [sem(f"xn_out{s}") for s in range(4)]
        var_ready = sem("var_ready")
        root_ready = sem("root_ready")
        norm_ready = sem("norm_ready")
        xn_made = sem("xn_made")
        turned = sem("turned")
        hi_made = sem("hi_made")
        lo_made = sem("lo_made")
        projected = sem("projected")
        proj_kept = sem("proj_kept")
        w_in = [sem(f"w_in{s}") for s in range(2)]
        w_hi_made = sem("w_hi_made")
        w_lo_made = sem("w_lo_made")
        bias_e_in = sem("bias_e_in")
        mask_ready = sem("mask_ready")
        counted = sem("counted")
        experts_known = sem("experts_known")
        hot_ready = sem("hot_ready")
        hot_used = sem("hot_used")
        tokens_found = sem("tokens_found")
        gather_ready = sem("gather_ready")
        rows_in = [sem(f"rows_in{s}") for s in range(4)]
        rows_turned = sem("rows_turned")
        rows_hi = sem("rows_hi")
        rows_lo = sem("rows_lo")
        y_made = sem("y_made")
        y_biased = sem("y_biased")
        y_done = sem("y_done")
        y_out = [sem(f"y_out{s}") for s in range(4)]
        heads_zero = sem("heads_zero")
        qk_laid = sem("qk_laid")
        v_laid = sem("v_laid")
        misc_filled = sem("misc_filled")
        misc_freed = sem("misc_freed")
        heads_in = [sem(f"heads_in{s}") for s in range(3)]
        scores_ready = sem("scores_ready")
        max_done = sem("max_done")
        max_laid = sem("max_laid")
        logits_ready = sem("logits_ready")
        exp_done = sem("exp_done")
        pv_done = sem("pv_done")
        o_kept = sem("o_kept")
        o_laid = sem("o_laid")
        acc_in = [sem(f"acc_in{s}") for s in range(4)]
        ya_in = [sem(f"ya_in{s}") for s in range(4)]
        yb_in = [sem(f"yb_in{s}") for s in range(4)]
        acc_ready = sem("acc_ready")
        acc_step = sem("acc_step")
        res_out = [sem(f"res_out{s}") for s in range(4)]

        misc = []

        def misc_plan(b, u):
            plan = {0: ([], [("o", b - 1, 1)]),
                    1: ([("max", b, 1)], [("k", b + 2, 0)]),
                    2: ([("turn", b - 1, 0)], [("k", b + 2, 1)]),
                    3: ([("out", b - 1, 0)], [("q", b + 2, 0)]),
                    4: ([("out", b - 1, 1)], [("q", b + 2, 1)]),
                    5: ([("out", b - 1, 2)], []),
                    6: ([("out", b - 1, 3)], [("o", b, 0)]),
                    7: ([("max", b + 1, 0)], [])}[u]
            return [[j for j in half if 0 <= j[1] < B] for half in plan]

        FIRST = [("k", 0, 0), ("k", 0, 1), ("q", 0, 0), ("q", 0, 1)]
        SECOND = [("k", 1, 0), ("k", 1, 1), ("q", 1, 0), ("q", 1, 1), ("max", 0, 0)]
        LAST = [("o", B - 1, 1), ("turn", B - 1, 0)] + [("out", B - 1, i) for i in range(QT)]
        misc += FIRST + SECOND
        for b in range(B):
            for u in range(2 * HG):
                for half in misc_plan(b, u):
                    misc += half
        misc += LAST
        misc_no = {job: n for n, job in enumerate(misc)}

        def result_made(i):
            return misc_no[("out", i // QT, i % QT)] + 1

        block = ctx.enter_context(nc.Block())

        @block.sync
        def _(sp):
            sp.dma_start(row_mid[:, 0, :], wqk).then_inc(weights_in, 16)
            sp.dma_start(row_mid[0:HD, 1, :], wv).then_inc(weights_in, 16)
            wo_src = wo.rearrange("(c p) k -> p c k", p=P)
            wo_dst = row_mid[:, 2, :].rearrange("p (c k) -> p c k", c=KC)
            sp.dma_start(wo_dst[:, :, 0:HD], wo_src).then_inc(weights_in, 16)
            sp.dma_start(wo_dst[:, :, HD:2 * HD], wo_src).then_inc(weights_in, 16)
            sp.dma_start(gate_w[:], wg.rearrange("(c p) e -> p c e", p=P)).then_inc(weights_in, 16)

            def load_x(i):
                if i >= 4:
                    sp.wait_ge(xn_made, i - 3)
                sp.dma_start(row_in[:, i % 4, :], x_rows[i * P:(i + 1) * P, :]).then_inc(x_in[i % 4], 16)

            def load_w(c):
                if c >= 2:
                    sp.wait_ge(w_lo_made, c - 1)
                e, half = divmod(c, 2)
                src = we[e].rearrange("(c p) h -> p c h", p=P)[:, 2 * half:2 * half + 2, :]
                sp.dma_start(stage[:, c % 2, :, :], src).then_inc(w_in[c % 2], 16)

            for i in range(4):
                load_x(i)

            def row(ap):
                return ap.rearrange("(a d) -> a d", a=1).to_broadcast([P, ap.shape[0]])

            sp.dma_start(bias_p[:, 0:2 * HD], row(bqk)).then_inc(biases_in, 16)
            sp.dma_start(bias_p[:, 2 * HD:3 * HD], row(bv)).then_inc(biases_in, 16)
            sp.dma_start(bias_p[:, 3 * HD:PW], row(bg)).then_inc(biases_in, 16)
            sp.dma_start(bias_o[:], row(bo)).then_inc(biases_in, 16)
            load_w(0)
            load_w(1)
            for i in range(NT):
                sp.wait_ge(xn_made, i + 1)
                sp.dma_start(xn_dram[i * P:(i + 1) * P, :], row_mid[:, i % 4, :]).then_inc(xn_out[i % 4], 16)
                if i + 4 < NT:
                    load_x(i + 4)
                if 2 <= i:
                    load_w(i)
            sp.wait_ge(projected, NT)
            sp.wait_ge(w_lo_made, 2 * NE)
            sp.wait_ge(w_hi_made, 2 * NE)
            sp.dma_start(bias_e[:], be.rearrange("(a e) h -> a e h", a=1).to_broadcast([P, NE, F])).then_inc(bias_e_in, 16)

            for n in range(NS):
                sp.wait_ge(y_done, n + 1)
                sp.dma_start(y_dram[n * P:(n + 1) * P, :], row_mid[:, n % 4, :]).then_inc(y_out[n % 4], 16)

            def load_acc(i):
                if i >= 4:
                    sp.wait_ge(misc_freed, result_made(i - 4))
                sp.dma_start(acc[:, i % 4, :], x_rows[i * P:(i + 1) * P, :]).then_inc(acc_in[i % 4], 16)

            def load_heads(b, g):
                sp.wait_ge(misc_freed, misc_no[("k", b, g)] + 1)
                if b == 0 and g == 0:
                    sp.wait_ge(heads_zero, 3)
                if b >= 3:
                    sp.wait_ge(logits_ready, (b - 2) * 2 * HG * HG)
                for j in range(HG):
                    rows = slice(32 * j, 32 * j + 32)
                    sp.dma_start(k_head[rows, b % 3, g * HG + j, :].bitcast(F32), k_t[rows, b % 2, g, :].bitcast(F32)).then_inc(heads_in[b % 3], 16)

            sp.wait_ge(y_biased, NS)
            sp.wait_ge(y_done, NS)
            sp.wait_ge(y_made, NS)
            for i in range(4):
                load_acc(i)
            for b in range(2):
                for g in range(G):
                    load_heads(b, g)
            for b in range(2, B + 2):
                if b < B:
                    for g in range(G):
                        load_heads(b, g)
                if b >= 3:
                    for i in range(QT * (b - 3), QT * (b - 2)):
                        sp.wait_ge(misc_freed, result_made(i))
                        sp.dma_start(out_rows[i * P:(i + 1) * P, :], res[:, i % 4, :]).then_inc(res_out[i % 4], 16)
                        if i + 4 < NT:
                            load_acc(i + 4)
            for i in range(QT * (B - 1), NT):
                sp.wait_ge(misc_freed, result_made(i))
                sp.dma_start(out_rows[i * P:(i + 1) * P, :], res[:, i % 4, :]).then_inc(res_out[i % 4], 16)
            for s in range(4):
                sp.wait_ge(res_out[s], 16 * NT // 4)

        @block.gpsimd
        def _(pool):
            steps = [0]

            def link(ins):
                steps[0] += 1
                ins.then_inc(pool_step, 1)
                pool.wait_ge(pool_step, steps[0])

            link(pool.memset(ident[:], 0.0))
            pool.affine_select(out=ident[:], in_=ident[:], compare_op=ALU.not_equal, fill=1.0, base=0,
                               pattern=[[-1, P]], channel_multiplier=1).then_inc(consts_ready, 1)
            pool.memset(eps_t[:], EPS).then_inc(consts_ready, 1)
            link(pool.memset(ones[:], 1.0))
            pool.affine_select(out=before[:], in_=ones[:], compare_op=ALU.is_gt, fill=0.0, base=0,
                               pattern=[[1, P]], channel_multiplier=-1).then_inc(consts_ready, 1)
            link(pool.iota(ramp_i[:], pattern=[[1, P]], base=0, channel_multiplier=0))
            pool.tensor_copy(ramp[:], ramp_i[:]).then_inc(consts_ready, 1)
            link(pool.iota(part_i[:], pattern=[[0, 1]], base=0, channel_multiplier=1))
            pool.tensor_copy(part[:], part_i[:]).then_inc(consts_ready, 1)
            link(pool.memset(lower[:], 1.0))
            pool.affine_select(out=lower[:], in_=lower[:], compare_op=ALU.is_gt, fill=0.0, base=0,
                               pattern=[[1, NE], [-1, NE]], channel_multiplier=0).then_inc(consts_ready, 1)

            for c in range(2 * NE):
                e, half = divmod(c, 2)
                pool.wait_ge(w_in[c % 2], 16 * (c // 2 + 1))
                pool.wait_ge(w_hi_made, c + 1)
                cs = slice(2 * half, 2 * half + 2)
                pool.tensor_tensor(w_lo[:, e, cs, :], stage[:, c % 2, :, :], w_hi[:, e, cs, :].bitcast(F32),
                                   ALU.subtract).then_inc(w_lo_made, 1)

            for s in range(4):
                pool.wait_ge(xn_out[s], 16 * NT // 4)
            pool.wait_ge(xn_made, NT)
            pool.wait_ge(gather_ready, 1)
            for n in range(NS):
                if n >= 4:
                    pool.wait_ge(rows_turned, n - 3)
                pool.indirect_dma_start(row_in[:, n % 4, :], None, xn_dram,
                                        bass.IndirectOffsetOnAxis(ap=gather_i[:, n:n + 1], axis=0)).then_inc(rows_in[n % 4], 16)

            pool.wait_ge(y_made, NS)
            pool.wait_ge(y_biased, NS)
            pool.memset(k_head[:, 1, :, :].bitcast(F32), 0.0).then_inc(heads_zero, 1)
            pool.memset(k_head[:, 2, :, :].bitcast(F32), 0.0).then_inc(heads_zero, 1)
            for s in range(4):
                pool.wait_ge(y_out[s], 16 * ((NS - s + 3) // 4))

            def fetch(i):
                if i >= 4:
                    pool.wait_ge(acc_ready, i - 3)
                for r, (dst, landed) in enumerate(((y_a, ya_in), (y_b, yb_in))):
                    pool.indirect_dma_start(dst[:, i % 4, :], None, y_dram,
                                            bass.IndirectOffsetOnAxis(ap=slots_i[:, r, i:i + 1], axis=0)).then_inc(landed[i % 4], 16)

            for i in range(3):
                fetch(i)
            for i in range(NT):
                s = i % 4
                if i + 3 < NT:
                    fetch(i + 3)
                pool.wait_ge(acc_in[s], 16 * (i // 4 + 1))
                if i == 0:
                    pool.wait_ge(biases_in, 64)
                pool.tensor_tensor(acc[:, s, :], acc[:, s, :], bias_o[:], ALU.add).then_inc(acc_step, 1)
                pool.wait_ge(ya_in[s], 16 * (i // 4 + 1))
                pool.wait_ge(yb_in[s], 16 * (i // 4 + 1))
                pool.tensor_tensor(y_a[:, s, :], y_a[:, s, :], y_b[:, s, :], ALU.add).then_inc(acc_step, 1)
                pool.wait_ge(acc_step, 2 * i + 2)
                pool.tensor_tensor(acc[:, s, :], acc[:, s, :], y_a[:, s, :], ALU.add).then_inc(acc_ready, 1)

        @block.scalar
        def _(act):
            act.wait_ge(consts_ready, 2)
            act.wait_ge(weights_turned, 1)
            act.activation(wo_hi[:], ps_m[:], ACT.Copy).then_inc(weights_split, 1)

            def split_w(c):
                e, half = divmod(c, 2)
                act.wait_ge(w_in[c % 2], 16 * (c // 2 + 1))
                act.activation(w_hi[:, e, 2 * half:2 * half + 2, :], stage[:, c % 2, :, :],
                               ACT.Copy).then_inc(w_hi_made, 1)

            def hi(i):
                act.wait_ge(turned, i + 1)
                if i >= 2:
                    act.wait_ge(projected, i - 1)
                act.activation(t_hi[:, i % 2, :], ps_t[:, i % 2, :], ACT.Copy).then_inc(hi_made, 1)

            for i in range(NT):
                if i % 2 == 0:
                    act.wait_ge(var_ready, i // 2 + 1)
                    act.activation(small[:, 1, i:i + 2], small[:, 0, i:i + 2], ACT.Sqrt).then_inc(root_ready, 1)
                    act.wait_ge(norm_ready, i // 2 + 1)
                act.wait_ge(x_in[i % 4], 16 * (i // 4 + 1))
                if i == 0:
                    act.wait_ge(weights_turned, 2)
                if i >= 4:
                    act.wait_ge(turned, i - 3)
                    act.wait_ge(xn_out[i % 4], 16 * (i // 4))
                act.activation(row_mid[:, i % 4, :], row_in[:, i % 4, :], ACT.Identity,
                               bias=small[:, 6, i:i + 1], scale=small[:, 5, i:i + 1]).then_inc(xn_made, 1)
                if i >= 1:
                    hi(i - 1)
                split_w(i)
            hi(NT - 1)

            def rows_high(n):
                act.wait_ge(rows_turned, n + 1)
                if n >= 2:
                    act.wait_ge(y_made, n - 1)
                act.activation(t_hi[:, n % 2, :], ps_t[:, n % 2, :], ACT.Copy).then_inc(rows_hi, 1)

            for n in range(NS):
                rows_high(n)
                if n >= 1:
                    act.wait_ge(y_biased, n)
                    act.activation(row_mid[:, (n - 1) % 4, :], row_mid[:, (n - 1) % 4, :], ACT.Relu,
                                   scale=0.5).then_inc(y_done, 1)
            act.wait_ge(y_biased, NS)
            act.activation(row_mid[:, (NS - 1) % 4, :], row_mid[:, (NS - 1) % 4, :], ACT.Relu,
                           scale=0.5).then_inc(y_done, 1)

            def keep(kind, b, g):
                m = misc_no[(kind, b, g)]
                act.wait_ge(misc_filled, m + 1)
                if kind == "k":
                    if b >= 2:
                        act.wait_ge(heads_in[(b - 2) % 3], 16 * H * ((b - 2) // 3 + 1))
                    dst = k_t[:, b % 2, g, :]
                elif kind == "q":
                    if b >= 2:
                        act.wait_ge(misc_freed, misc_no[("max", b - 2, G - 1)] + 1)
                        act.wait_ge(scores_ready, (b - 1) * 2 * H)
                    dst = q_t[:, b % 2, g, :]
                else:
                    if b >= 1:
                        act.wait_ge(misc_filled, misc_no[("out", b - 1, QT - 1)] + 1)
                    dst = o_t[:]
                act.activation(dst, ps_m[:], ACT.Copy).then_inc(misc_freed, 1)

            for job in FIRST + SECOND[:-1]:
                keep(*job)

            def keep_o(b, g):
                act.wait_ge(pv_done, 2 * HG * b + HG * (g + 1))
                if 2 * b + g >= 2:
                    act.wait_ge(misc_filled, misc_no[("o", b - 1, g)] + 1)
                act.activation(o_sum[:, g, :], ps_o[:], ACT.Copy).then_inc(o_kept, 1)

            for b in range(B):
                for u in range(2 * HG):
                    n = 2 * HG * b + u
                    mid, end = misc_plan(b, u)
                    for j in range(HG):
                        act.wait_ge(logits_ready, HG * n + j + 1)
                        if j == 0 and n >= 2:
                            act.wait_ge(pv_done, n - 1)
                        act.activation(probs[:, n % 2, j, :], ps_t[:, j % 2, :], ACT.Exp).then_inc(exp_done, 1)
                        if j == 1:
                            if u == 0 and b >= 1:
                                keep_o(b - 1, 1)
                            if u == HG:
                                keep_o(b, 0)
                            for job in mid:
                                if job[0] in ("k", "q", "turn"):
                                    keep(*job)
                    for job in end:
                        if job[0] in ("k", "q", "turn"):
                            keep(*job)
            keep_o(B - 1, 1)
            keep("turn", B - 1, 0)

        @block.vector
        def _(dve):
            steps = [0]

            def link(ins):
                steps[0] += 1
                ins.then_inc(dve_step, 1)
                dve.wait_ge(dve_step, steps[0])

            dve.memset(ps_o[:], 0.0).then_inc(dve_step, 1)
            steps[0] += 1
            dve.wait_ge(weights_turned, 1)
            dve.wait_ge(weights_split, 1)
            dve.tensor_tensor(wo_lo[:], ps_m[:], wo_hi[:].bitcast(F32), ALU.subtract).then_inc(weights_split, 1)
            dve.wait_ge(weights_turned, 2)
            dve.wait_ge(weights_in, 80)
            wp_ps = ps_s[:, 2:4, :].rearrange("p a (c n) -> p (a c) n", c=2)
            link(dve.tensor_copy(wp_hi[:, :, 0:3 * HD], wp_ps[:, :, 0:3 * HD]))
            link(dve.tensor_copy(wp_hi[:, :, 3 * HD:PW], gate_w[:]))
            dve.tensor_tensor(wp_lo[:, :, 0:3 * HD], wp_ps[:, :, 0:3 * HD], wp_hi[:, :, 0:3 * HD].bitcast(F32),
                              ALU.subtract).then_inc(weights_split, 1)
            dve.tensor_tensor(wp_lo[:, :, 3 * HD:PW], gate_w[:], wp_hi[:, :, 3 * HD:PW].bitcast(F32),
                              ALU.subtract).then_inc(weights_split, 1)

            def moments(g):
                for i in (2 * g, 2 * g + 1):
                    dve.wait_ge(x_in[i % 4], 16 * (i // 4 + 1))
                    dve.bn_stats(stats[:, g % 2, i % 2, :], row_in[:, i % 4, :]).then_inc(dve_step, 1)
                    steps[0] += 1
                for i in (2 * g, 2 * g + 1):
                    dve.wait_ge(dve_step, steps[0] - 1 + i % 2 if i % 2 else steps[0] - 1)
                    dve.bn_aggr(mv[:, i, :], stats[:, g % 2, i % 2, :]).then_inc(dve_step, 1)
                    steps[0] += 1
                dve.wait_ge(dve_step, steps[0])
                ts = slice(2 * g, 2 * g + 2)
                dve.tensor_scalar(small[:, 0, ts], mv[:, ts, 1], EPS, None, ALU.add).then_inc(var_ready, 1)

            def scales(g):
                ts = slice(2 * g, 2 * g + 2)
                d, r, a, c = (small[:, k, ts] for k in (0, 2, 3, 4))
                dve.wait_ge(var_ready, g + 1)
                dve.wait_ge(root_ready, g + 1)
                link(dve.reciprocal(r, small[:, 1, ts]))
                link(dve.tensor_tensor(a, r, r, ALU.mult))
                link(dve.tensor_tensor(c, a, d, ALU.mult))
                link(dve.tensor_scalar(a, c, -0.5, 1.5, ALU.mult, ALU.add))
                link(dve.tensor_tensor(small[:, 5, ts], r, a, ALU.mult))
                dve.scalar_tensor_tensor(out=small[:, 6, ts], in0=mv[:, ts, 0], scalar=-1.0,
                                         in1=small[:, 5, ts], op0=ALU.mult, op1=ALU.mult).then_inc(norm_ready, 1)

            def low(i):
                dve.wait_ge(hi_made, i + 1)
                if i >= 2:
                    dve.wait_ge(projected, i - 1)
                dve.tensor_tensor(t_lo[:, i % 2, :], ps_t[:, i % 2, :], t_hi[:, i % 2, :].bitcast(F32),
                                  ALU.subtract).then_inc(lo_made, 1)

            def keep_proj(i):
                dve.wait_ge(projected, i + 1)
                if i == 0:
                    dve.wait_ge(biases_in, 64)
                dve.tensor_tensor(proj[:, i, :], ps_s[:, i % 2, 0:PW], bias_p[:], ALU.add).then_inc(proj_kept, 1)

            def top(i):
                dve.wait_ge(proj_kept, i + 1)
                logits = proj[:, i, 3 * HD:PW]
                link(dve.max(top_v[:, i, :], logits))
                dve.max_index(top_i[:, i, :], top_v[:, i, :], logits).then_inc(dve_step, 1)
                steps[0] += 1

            moments(0)
            scales(0)
            for i in range(NT):
                if i % 2 == 0 and i + 2 < NT:
                    moments(i // 2 + 1)
                low(i)
                if i >= 1:
                    keep_proj(i - 1)
                if i % 2 == 0 and i + 2 < NT:
                    scales(i // 2 + 1)
                if i >= 1:
                    top(i - 1)
            keep_proj(NT - 1)
            top(NT - 1)

            dve.wait_ge(dve_step, steps[0])
            link(dve.tensor_copy(top_f[:], top_i[:]))
            dve.wait_ge(consts_ready, 6)
            ramp8 = ramp[:, 0:NE].unsqueeze(1).to_broadcast([P, NT, NE])
            for r in range(2):
                ins = dve.tensor_tensor(pick[:, r], ramp8, top_f[:, :, r:r + 1].to_broadcast([P, NT, NE]), ALU.is_equal)
                ins.then_inc(dve_step, 1)
                steps[0] += 1
            dve.memset(mask[:, NT, :], 0.0).then_inc(mask_ready, 1)
            dve.wait_ge(dve_step, steps[0])
            dve.tensor_tensor(mask[:, 0:NT, :], pick[:, 0], pick[:, 1], ALU.add).then_inc(mask_ready, 1)

            dve.wait_ge(counted, 1)
            ps_c = ps_m[:, 0:(NT + 1) * NE].rearrange("p (i e) -> p i e", e=NE)
            link(dve.tensor_copy(place[:], ps_c))
            thresholds = ramp[:, 0:NT].unsqueeze(1).to_broadcast([P, NE, NT])
            counts = ecol[:, 0, :]
            link(dve.tensor_scalar(counts, place[:, NT, :], 1.0 / P, None, ALU.mult))
            link(dve.tensor_tensor(tiles_gt[:], counts.unsqueeze(2).to_broadcast([P, NE, NT]), thresholds, ALU.is_gt))
            link(dve.tensor_reduce(ecol[:, 1, :], tiles_gt[:], AX.X, ALU.add))
            link(dve.tensor_tensor(tri[:], lower[:], ecol[:, 1:2, :].to_broadcast([P, NE, NE]), ALU.mult))
            link(dve.tensor_reduce(ecol[:, 2, :], tri[:], AX.X, ALU.add))
            link(dve.tensor_tensor(ecol[:, 3, :], ecol[:, 1, :], ecol[:, 2, :], ALU.add))
            link(dve.tensor_scalar(ecol[:, 0, :], ecol[:, 2, :], float(P), None, ALU.mult))
            link(dve.tensor_tensor(place[:, 0:NT, :], place[:, 0:NT, :], ecol[:, 0:1, :].to_broadcast([P, NT, NE]), ALU.add))
            for r in range(2):
                link(dve.tensor_tensor(slot_p[:, r], place[:, 0:NT, :], pick[:, r], ALU.mult))
            link(dve.tensor_reduce(slot_f[:], slot_p[:], AX.X, ALU.add))
            link(dve.tensor_copy(slots_i[:], slot_f[:]))
            link(dve.tensor_scalar(slot_r[:, 0], slots_i[:], P - 1, None, ALU.bitwise_and))
            link(dve.tensor_scalar(slot_r[:, 1], slots_i[:], P.bit_length() - 1, None, ALU.arith_shift_right))
            link(dve.tensor_copy(slot_q[:], slot_r[:].rearrange("p a r i -> p a (r i)")))
            ramp_s = ramp[:, 0:NS].unsqueeze(1).to_broadcast([P, NC, NS])
            link(dve.tensor_tensor(hot_tile[:], ramp_s, slot_q[:, 1, :].unsqueeze(2).to_broadcast([P, NC, NS]), ALU.is_equal))
            for r in range(2):
                tile_no = ramp[:, 0:NT].unsqueeze(2).to_broadcast([P, NT, NS])
                cs = slice(r * NT, (r + 1) * NT)
                dve.tensor_tensor(hot_val[:, cs, 0, :], hot_tile[:, cs, :], tile_no, ALU.mult).then_inc(hot_ready, 1)
            dve.tensor_scalar(hot_val[:, :, 1, :], hot_tile[:], part[:, 0:1], None, ALU.mult).then_inc(hot_ready, 1)
            for c in range(NC // 4):
                if c >= 2:
                    dve.wait_ge(hot_used, c - 1)
                ramp_r = ramp[:].unsqueeze(1).to_broadcast([P, 4, P])
                slot_row = slot_q[:, 0, 4 * c:4 * c + 4].unsqueeze(2).to_broadcast([P, 4, P])
                dve.tensor_tensor(hot_row[:, c % 2], ramp_r, slot_row, ALU.is_equal).then_inc(hot_ready, 1)
            link(dve.tensor_tensor(te_cmp[:], ecol[:, 3:4, :].to_broadcast([P, NS, NE]),
                                   ramp[:, 0:NS].unsqueeze(2).to_broadcast([P, NS, NE]), ALU.is_le))
            link(dve.tensor_reduce(te_f[:], te_cmp[:], AX.X, ALU.add))
            dve.tensor_scalar(expert_i[:], te_f[:], float(NE - 1), None, ALU.min).then_inc(experts_known, 1)
            dve.wait_ge(tokens_found, 1)
            found = ps_s[:, 3, 0:2 * NS].rearrange("p (a n) -> p a n", a=2)
            link(dve.tensor_copy(tok_f[:], found))
            dve.scalar_tensor_tensor(out=gather_i[:], in0=tok_f[:, 0, :], scalar=float(P), in1=tok_f[:, 1, :],
                                     op0=ALU.mult, op1=ALU.add).then_inc(gather_ready, 1)

            def rows_low(n):
                dve.wait_ge(rows_hi, n + 1)
                dve.tensor_tensor(t_lo[:, n % 2, :], ps_t[:, n % 2, :], t_hi[:, n % 2, :].bitcast(F32),
                                  ALU.subtract).then_inc(rows_lo, 1)

            dve.wait_ge(experts_known, 1)
            dve.wait_ge(bias_e_in, 16)
            for n in range(NS + 1):
                if n < NS:
                    rows_low(n)
                if n >= 1:
                    e = dve.value_load(expert_i[0:1, n - 1:n], min_val=0, max_val=NE - 1)
                    dve.wait_ge(y_made, n)
                    if n > 4:
                        dve.wait_ge(y_out[(n - 1) % 4], 16 * ((n - 1) // 4))
                    dve.tensor_tensor(row_mid[:, (n - 1) % 4, :], ps_s[:, (n - 1) % 2, :], bias_e[:, bass.ds(e, 1), :].rearrange("p a h -> p (a h)"),
                                      ALU.add).then_inc(y_biased, 1)

            dve.wait_ge(y_biased, NS)
            dve.memset(k_head[:, 0, :, :].bitcast(F32), 0.0).then_inc(heads_zero, 1)
            link(dve.memset(a_q[:], 0.0))
            link(dve.memset(a_k[:], 0.0))
            link(dve.memset(a_m[:], 0.0))
            heads_q = a_q[:].rearrange("p i (h c) -> p i h c", c=32)
            heads_k = a_k[:].rearrange("p i (h c) -> p i h c", c=32)
            heads_m = a_m[:].rearrange("p i (h c) -> p i h c", c=32)
            link(dve.memset(heads_k[:, :, :, 0:2], 1.0))
            link(dve.memset(v_ones[:, :, :, HE:VC], float(HD) ** 0.5))
            dve.wait_ge(dve_step, steps[0])

            def lay_qk(b):
                src = proj[:, QT * b:QT * (b + 1), 0:2 * HD].rearrange("p i (h e s) -> p i h e s", e=HE, s=2)
                if b >= 1:
                    dve.wait_ge(misc_filled, misc_no[("q", b - 1, G - 1)] + 1)
                for s, heads, hi_at, lo_at in ((0, heads_q, (2, 10), 18), (1, heads_k, (2, 18), 10)):
                    exact = src[:, :, :, :, s]
                    hi = heads[:, :, :, hi_at[0]:hi_at[0] + HE]
                    for i in range(QT):
                        dve.tensor_copy(hi[:, i].bitcast(F32R), exact[:, i]).then_inc(dve_step, 1)
                        dve.tensor_copy(heads[:, i, :, hi_at[1]:hi_at[1] + HE].bitcast(F32R), exact[:, i]).then_inc(dve_step, 1)
                        steps[0] += 2
                    dve.wait_ge(dve_step, steps[0])
                    for i in range(QT):
                        dve.tensor_tensor(heads[:, i, :, lo_at:lo_at + HE], exact[:, i], hi[:, i], ALU.subtract).then_inc(qk_laid, 1)
                dve.tensor_copy(v_ones[:, QT * b:QT * (b + 1), :, 0:HE],
                                proj[:, QT * b:QT * (b + 1), 2 * HD:3 * HD].rearrange("p i (h e) -> p i h e", e=HE)).then_inc(v_laid, 1)

            def maxima(b, h):
                for half in range(2):
                    n = 2 * (H * b + h) + half
                    dve.wait_ge(scores_ready, n + 1)
                    if b >= 2 and h == 0 and half == 0:
                        dve.wait_ge(max_laid, 2 * (b - 1))
                    dve.tensor_reduce(row_max[:, b % 2, h, 2 * half:2 * half + 2], ps_s[:, 2 * half:2 * half + 2, :],
                                      AX.X, ALU.max).then_inc(max_done, 1)

            def lay_max(b, g):
                dve.wait_ge(max_done, 2 * H * b + 2 * HG * (g + 1))
                if b >= 1:
                    dve.wait_ge(misc_filled, misc_no[("max", b - 1, g)] + 1)
                mx = row_max[:, b % 2, HG * g:HG * (g + 1), :].rearrange("p h i -> p i h")
                hs = slice(HG * g, HG * (g + 1))
                link(dve.tensor_scalar(heads_m[:, :, hs, 0].bitcast(F32R), mx, -1.0, None, ALU.mult))
                dve.scalar_tensor_tensor(out=heads_m[:, :, hs, 1], in0=mx, scalar=-1.0, in1=heads_m[:, :, hs, 0],
                                         op0=ALU.mult, op1=ALU.subtract).then_inc(max_laid, 1)

            def add_max(b, g):
                m = misc_no[("max", b, g)]
                dve.wait_ge(misc_filled, m + 1)
                if b >= 1:
                    dve.wait_ge(logits_ready, HG * (2 * HG * (b - 1) + HG * (g + 1)))
                dve.wait_ge(misc_freed, misc_no[("q", b, g)] + 1)
                dve.tensor_tensor(q_m[:, g, :], ps_m[:], q_t[:, b % 2, g, :].bitcast(F32), ALU.add).then_inc(misc_freed, 1)

            def lay_o(b, g):
                m = misc_no[("o", b, g)]
                dve.wait_ge(misc_filled, m + 1)
                sums = ps_m[:].rearrange("p (i j c) -> p i j c", j=HG, c=32)
                if b >= 1 and g == 0:
                    dve.wait_ge(misc_filled, misc_no[("turn", b - 1, 0)] + 1)
                link(dve.reciprocal(o_inv[:], sums[:, :, :, HE]))
                cs = slice(g * HG * HE, (g + 1) * HG * HE)
                exact = o_exact[:, :, cs].rearrange("p i (j e) -> p i j e", e=HE)
                steps[0] += 1
                for i in range(QT):
                    ins = dve.tensor_tensor(exact[:, i], sums[:, i, :, 0:HE], o_inv[:, i, :].unsqueeze(2).to_broadcast([P, HG, HE]), ALU.mult)
                    if i < QT - 1:
                        ins.then_inc(dve_step, 1)
                        steps[0] += 1
                steps[0] -= 1
                ins.then_inc(misc_freed, 1)
                dve.wait_ge(dve_step, steps[0])
                dve.wait_ge(misc_freed, m + 1)
                link(dve.tensor_copy(o_tok[:, :, cs].bitcast(F32R), o_exact[:, :, cs]))
                dve.tensor_tensor(o_tok[:, :, HD + g * HG * HE:HD + (g + 1) * HG * HE], o_exact[:, :, cs],
                                  o_tok[:, :, cs], ALU.subtract).then_inc(o_laid, 1)

            def result(b, i):
                n = QT * b + i
                m = misc_no[("out", b, i)]
                dve.wait_ge(acc_ready, n + 1)
                if n >= 4:
                    dve.wait_ge(res_out[n % 4], 16 * (n // 4))
                dve.wait_ge(misc_filled, m + 1)
                dve.tensor_tensor(res[:, n % 4, :], ps_m[:], acc[:, n % 4, :], ALU.add).then_inc(misc_freed, 1)

            def serve(jobs):
                for kind, b, g in jobs:
                    if kind == "max":
                        add_max(b, g)
                    elif kind == "o":
                        lay_o(b, g)
                    elif kind == "out":
                        result(b, g)

            lay_qk(0)
            lay_qk(1)
            for h in range(H):
                maxima(0, h)
            lay_max(0, 0)
            add_max(0, 0)
            lay_max(0, 1)
            for b in range(B):
                for u in range(2 * HG):
                    mid, end = misc_plan(b, u)
                    if u == 0 and b + 2 < B:
                        lay_qk(b + 2)
                    if b + 1 < B:
                        maxima(b + 1, u)
                    if u == 3 and b + 1 < B:
                        lay_max(b + 1, 0)
                    if u == 7 and b + 1 < B:
                        lay_max(b + 1, 1)
                    serve(mid)
                    serve(end)
            serve(LAST)

        @block.tensor
        def _(pe):
            pe.wait_ge(consts_ready, 1)
            pe.wait_ge(weights_in, 80)
            for c in range(KC):
                mm = pe.transpose(ps_m[:, c * P:(c + 1) * P], row_mid[:, 2, c * P:(c + 1) * P], ident[:])
            mm.then_inc(weights_turned, 1)
            wp_ps = ps_s[:, 2:4, :].rearrange("p a (c n) -> p (a c) n", c=2)
            for c in range(KC):
                pe.transpose(wp_ps[:, c, 0:P], row_mid[:, 0, c * P:(c + 1) * P], ident[:])
                mm = pe.transpose(wp_ps[:, c, P:P + HD], row_mid[0:HD, 1, c * P:(c + 1) * P], ident[0:HD, 0:HD])
            mm.then_inc(weights_turned, 1)

            def turn(i):
                pe.wait_ge(xn_made, i + 1)
                if i >= 2:
                    pe.wait_ge(lo_made, i - 1)
                for c in range(KC):
                    mm = pe.transpose(ps_t[:, i % 2, c * P:(c + 1) * P], row_mid[:, i % 4, c * P:(c + 1) * P], ident[:])
                mm.then_inc(turned, 1)

            def project(i):
                pe.wait_ge(hi_made, i + 1)
                pe.wait_ge(lo_made, i + 1)
                if i == 0:
                    pe.wait_ge(weights_split, 4)
                if i >= 2:
                    pe.wait_ge(proj_kept, i - 1)
                n = 0
                for c in range(KC):
                    ks = slice(c * P, (c + 1) * P)
                    for a, w in ((t_hi, wp_hi), (t_hi, wp_lo), (t_lo, wp_hi)):
                        mm = pe.matmul(ps_s[:, i % 2, 0:PW], a[:, i % 2, ks], w[:, c, :], start=(n == 0), stop=(n == 3 * KC - 1))
                        n += 1
                mm.then_inc(projected, 1)

            for i in range(NT):
                turn(i)
                if i >= 1:
                    project(i - 1)
            project(NT - 1)

            pe.wait_ge(mask_ready, 2)
            counts = ps_m[:, 0:(NT + 1) * NE].rearrange("p (i e) -> p i e", e=NE)
            pe.matmul(counts[:, :, :], before[:], mask[:, :, :], start=True, stop=False)
            for i in range(NT):
                later = NT - i
                mm = pe.matmul(counts[:, i + 1:NT + 1, :], ones[:], mask[:, i:i + 1, :].to_broadcast([P, later, NE]),
                               start=False, stop=(i == NT - 1))
            mm.then_inc(counted, 1)
            pe.wait_ge(hot_ready, 3)
            for c in range(NC):
                if c % 4 == 0:
                    pe.wait_ge(hot_ready, 4 + c // 4)
                mm = pe.matmul(ps_s[:, 3, 0:2 * NS], hot_row[:, (c // 4) % 2, c % 4, :], hot_val[:, c].rearrange("p a n -> p (a n)"),
                               start=(c == 0), stop=(c == NC - 1))
                if c % 4 == 3 and c < NC - 1:
                    mm.then_inc(hot_used, 1)
            mm.then_inc(tokens_found, 1)

            def turn_rows(n):
                pe.wait_ge(rows_in[n % 4], 16 * (n // 4 + 1))
                if n >= 2:
                    pe.wait_ge(rows_lo, n - 1)
                for c in range(KC):
                    mm = pe.transpose(ps_t[:, n % 2, c * P:(c + 1) * P], row_in[:, n % 4, c * P:(c + 1) * P], ident[:])
                mm.then_inc(rows_turned, 1)

            pe.wait_ge(experts_known, 1)
            pe.wait_ge(w_hi_made, 2 * NE)
            pe.wait_ge(w_lo_made, 2 * NE)
            turn_rows(0)
            for n in range(NS):
                e = pe.value_load(expert_i[0:1, n:n + 1], min_val=0, max_val=NE - 1)
                if n + 1 < NS:
                    turn_rows(n + 1)
                pe.wait_ge(rows_hi, n + 1)
                pe.wait_ge(rows_lo, n + 1)
                if n >= 2:
                    pe.wait_ge(y_biased, n - 1)
                k = 0
                for c in range(KC):
                    ks = slice(c * P, (c + 1) * P)
                    for a, w in ((t_hi, w_hi), (t_hi, w_lo), (t_lo, w_hi)):
                        rhs = w[:, bass.ds(e, 1), c, :].rearrange("p a h -> p (a h)")
                        mm = pe.matmul(ps_s[:, n % 2, :], a[:, n % 2, ks], rhs, start=(k == 0), stop=(k == 3 * KC - 1))
                        k += 1
                mm.then_inc(y_made, 1)

            def fill(kind, b, g):
                m = misc_no[(kind, b, g)]
                if m >= 1:
                    pe.wait_ge(misc_freed, m)
                if kind in ("k", "q"):
                    pe.wait_ge(qk_laid, 2 * QT * (b + 1))
                    src = a_q if kind == "q" else a_k
                    for i in range(QT):
                        mm = pe.transpose(ps_m[:, i * P:(i + 1) * P], src[:, i, g * P:(g + 1) * P], ident[:])
                elif kind == "max":
                    pe.wait_ge(max_laid, 2 * b + g + 1)
                    for i in range(QT):
                        mm = pe.transpose(ps_m[:, i * P:(i + 1) * P], a_m[:, i, g * P:(g + 1) * P], ident[:])
                elif kind == "o":
                    pe.wait_ge(o_kept, 2 * b + g + 1)
                    for i in range(QT):
                        mm = pe.transpose(ps_m[:, i * P:(i + 1) * P], o_sum[:, g, i * P:(i + 1) * P], ident[:])
                elif kind == "turn":
                    pe.wait_ge(o_laid, 2 * b + 2)
                    for i in range(QT):
                        mm = pe.transpose(ps_m[:, i * P:(i + 1) * P], o_tok[:, i, :], ident[:])
                else:
                    pe.wait_ge(misc_freed, misc_no[("turn", b, 0)] + 1)
                    ts = slice(g * P, (g + 1) * P)
                    pe.matmul(ps_m[:], o_t[:, ts], wo_hi[:], start=True, stop=False)
                    mm = pe.matmul(ps_m[:], o_t[:, ts], wo_lo[:], start=False, stop=True)
                mm.then_inc(misc_filled, 1)

            def scores(b, h, half):
                n = 2 * (H * b + h) + half
                if half == 0 and h % HG == 0:
                    pe.wait_ge(heads_in[b % 3], 16 * H * (b // 3 + 1))
                    pe.wait_ge(misc_freed, misc_no[("q", b, h // HG)] + 1)
                if n >= 2:
                    pe.wait_ge(max_done, n - 1)
                for i in (2 * half, 2 * half + 1):
                    mm = pe.matmul(ps_s[:, i, :], q_t[:, b % 2, h // HG, i * P:(i + 1) * P], k_head[:, b % 3, h, :],
                                   start=True, stop=True)
                mm.then_inc(scores_ready, 1)

            def logits(b, u, j):
                g, kt = divmod(u, QT)
                n = HG * (2 * HG * b + u) + j
                if n >= 2:
                    pe.wait_ge(exp_done, n - 1)
                if kt == 0 and j == 0:
                    pe.wait_ge(misc_freed, misc_no[("max", b, g)] + 1)
                pe.matmul(ps_t[:, n % 2, :], k_head[:, b % 3, g * HG + j, kt * P:(kt + 1) * P], q_m[:, g, :],
                          start=True, stop=True).then_inc(logits_ready, 1)

            def values(b, u):
                g, kt = divmod(u, QT)
                n = 2 * HG * b + u
                pe.wait_ge(exp_done, HG * (n + 1))
                pe.wait_ge(v_laid, b + 1)
                if kt == 0 and n > 0:
                    pe.wait_ge(o_kept, 2 * b + g)
                for j in range(HG):
                    mm = pe.matmul(ps_o[32 * j:32 * j + VC, :], v_ones[:, QT * b + kt, g * HG + j, :], probs[:, n % 2, j, :],
                                   start=(kt == 0), stop=(kt == QT - 1))
                mm.then_inc(pv_done, 1)

            pe.wait_ge(y_biased, NS)
            for job in FIRST:
                fill(*job)
            for job in SECOND[:-1]:
                fill(*job)
            for h in range(H):
                for half in range(2):
                    scores(0, h, half)
            fill(*SECOND[-1])
            for b in range(B):
                for u in range(2 * HG):
                    mid, end = misc_plan(b, u)
                    logits(b, u, 0)
                    logits(b, u, 1)
                    if b + 1 < B:
                        scores(b + 1, u, 0)
                    if u >= 1:
                        values(b, u - 1)
                    elif b >= 1:
                        values(b - 1, 2 * HG - 1)
                    for job in mid:
                        fill(*job)
                    logits(b, u, 2)
                    logits(b, u, 3)
                    if b + 1 < B:
                        scores(b + 1, u, 1)
                    for job in end:
                        fill(*job)
            values(B - 1, 2 * HG - 1)
            for job in LAST:
                fill(*job)


_INS = ['L0_attn_x', 'L0_attn_Wqk_w', 'L0_attn_Wqk_b', 'L0_attn_Wv_w', 'L0_attn_Wv_b', 'L0_attn_Wo_w', 'L0_attn_Wo_b',
        'L0_ffn_W_gate', 'L0_ffn_b_gate', 'L0_ffn_W_e', 'L0_ffn_b_e']
_OUTS = [((B, N, D), 'float32')]


def kernel(**inputs):
    import numpy as _np
    import concourse.bacc as _bacc
    from concourse import mybir as _mybir
    from concourse.bass_utils import run_bass_kernel_spmd as _run

    nc = _bacc.Bacc("TRN2", target_bir_lowering=False, num_devices=1)
    arrays, args = {}, []
    for name in _INS:
        a = _np.ascontiguousarray(inputs[name])
        arrays[f"in_{name}_dram"] = a
        args.append(nc.dram_tensor(f"in_{name}_dram", a.shape, _mybir.dt.from_np(a.dtype), kind="ExternalInput").ap())
    for i, (shape, dtype) in enumerate(_OUTS):
        dt = _mybir.dt.from_np(_np.dtype(dtype))
        args.append(nc.dram_tensor(f"out_{i}_dram", shape, dt, kind="ExternalOutput").ap())
    attention_and_experts(nc, *args)
    r = _run(nc, [arrays], core_ids=[0])
    return r.results[0]["out_0_dram"]
```

```python
from contextlib import ExitStack

import concourse.bass as bass
from concourse import mybir

F32 = mybir.dt.float32
F32R = mybir.dt.float32r
BF16 = mybir.dt.bfloat16
I32 = mybir.dt.int32
U32 = mybir.dt.uint32
ALU = mybir.AluOpType
ACT = mybir.ActivationFunctionType
AX = mybir.AxisListType

P = 128
B, N, D = 4, 512, 512
T = B * N
NT = T // P
KC = D // P
H, HE = 8, 8
HD = H * HE
G = 2
HG = H // G
NE, F = 8, 512
PW = 3 * HD + NE
QT = N // P
NS = (2 * T + NE * (P - 1)) // P
NC = 2 * NT
EPS = 1e-5
VC = HE + 1
RI = 6
RW = 5
RA = 6


def attention_and_experts(nc, x, wqk, bqk, wv, bv, wo, bo, wg, bg, we, be, out):
    x_rows = x.rearrange("b n d -> (b n) d")
    out_rows = out.rearrange("b n d -> (b n) d")
    xn_dram = nc.dram_tensor("xn_rows", (T, D), F32).ap()
    y_dram = nc.dram_tensor("expert_rows", (NS * P, F), F32).ap()

    ctx = ExitStack()
    with ctx:
        def sb(name, shape, dt, where=ctx):
            return where.enter_context(nc.sbuf_tensor(name, shape, dt))

        def sem(name):
            return ctx.enter_context(nc.semaphore(name))

        ident = sb("ident", [P, P], F32)
        before = sb("before", [P, P], BF16)
        ones = sb("ones", [P, P], BF16)
        ramp_i = sb("ramp_i", [P, P], I32)
        ramp = sb("ramp", [P, P], F32)
        part_i = sb("part_i", [P, 1], I32)
        part = sb("part", [P, 1], F32)
        lower = sb("lower", [P, NE, NE], F32)
        eps_t = sb("eps_t", [P, 1], F32)
        bias_p = sb("bias_p", [P, PW], F32)
        bias_o = sb("bias_o", [P, D], F32)
        wo_hi = sb("wo_hi", [P, D], F32R)
        wo_lo = sb("wo_lo", [P, D], F32R)
        proj = sb("proj", [P, NT, PW], F32)
        slots_i = sb("slots_i", [P, 2, NT], I32)
        gather_i = sb("gather_i", [P, NS], I32)
        expert_i = sb("expert_i", [P, NS], I32)
        row_mid = sb("row_mid", [P, 4, D], F32)

        top_v = sb("top_v", [P, NT, 8], F32)
        top_i = sb("top_i", [P, NT, 8], U32)

        stats = sb("stats", [P, 2, 2, 6], F32)
        mv = sb("mv", [P, NT, 2], F32)
        small = sb("small", [P, 8, NT], F32)
        rows_era = ExitStack()
        row_in = sb("row_in", [P, RI, D], F32, rows_era)
        rows_era.close()
        rout = ExitStack()
        top_f = sb("top_f", [P, NT, 8], F32, rout)
        pick = sb("pick", [P, 2, NT, NE], F32, rout)
        mask = sb("mask", [P, NT + 1, NE], BF16, rout)
        place = sb("place", [P, NT + 1, NE], F32, rout)
        tiles_gt = sb("tiles_gt", [P, NE, NT], F32, rout)
        tri = sb("tri", [P, NE, NE], F32, rout)
        ecol = sb("ecol", [P, 4, NE], F32, rout)
        te_cmp = sb("te_cmp", [P, NS, NE], F32, rout)
        te_f = sb("te_f", [P, NS], F32, rout)
        slot_p = sb("slot_p", [P, 2, NT, NE], F32, rout)
        slot_f = sb("slot_f", [P, 2, NT], F32, rout)
        slot_r = sb("slot_r", [P, 2, 2, NT], I32, rout)
        slot_q = sb("slot_q", [P, 2, NC], F32, rout)
        hot_tile = sb("hot_tile", [P, NC, NS], BF16, rout)
        tok_f = sb("tok_f", [P, 2, NS], F32, rout)
        rout.close()
        sb("row_in_place", [P, RI, D], F32)
        turned_era = ExitStack()
        t_hi = sb("t_hi", [P, 2, D], F32R, turned_era)
        t_lo = sb("t_lo", [P, 2, D], F32R, turned_era)
        turned_era.close()
        hot_row = sb("hot_row", [P, 2, 4, P], BF16)
        hot_val = sb("hot_val", [P, NC, 2, NS], BF16)
        sb("hot_gap", [P, 4 * D - NC * NS - 4 * P], F32)

        era = ExitStack()
        w_hi = sb("w_hi", [P, NE, KC, F], F32R, era)
        w_lo = sb("w_lo", [P, NE, KC, F], F32R, era)
        sub = ExitStack()
        stage = sb("stage", [P, RW, 2, F], F32, sub)
        wp_hi = sb("wp_hi", [P, KC, PW], F32R, sub)
        wp_lo = sb("wp_lo", [P, KC, PW], F32R, sub)
        gate_w = sb("gate_w", [P, KC, NE], F32, sub)
        sub.close()
        bias_e = sb("bias_e", [P, NE, F], F32, era)
        era.close()
        att = ExitStack()
        a_q = sb("a_q", [P, QT, G * P], F32, att)
        a_k = sb("a_k", [P, QT, G * P], F32, att)
        a_m = sb("a_m", [P, QT, G * P], F32, att)
        v_ones = sb("v_ones", [P, NT, H, VC], F32, att)
        q_t = sb("q_t", [P, 2, G, N], F32R, att)
        k_t = sb("k_t", [P, 2, G, N], F32R, att)
        k_head = sb("k_head", [P, 3, H, N], F32R, att)
        q_m = sb("q_m", [P, G, N], F32R, att)
        row_max = sb("row_max", [P, 2, H, QT], F32, att)
        probs = sb("probs", [P, 2, HG, N], F32, att)
        o_sum = sb("o_sum", [P, 2, N], F32, att)
        o_inv = sb("o_inv", [P, QT, HG], F32, att)
        o_tok = sb("o_tok", [P, QT, P], F32, att)
        o_exact = sb("o_exact", [P, QT, HD], F32, att)
        o_t = sb("o_t", [P, N], F32R, att)
        acc = sb("acc", [P, RA, D], F32, att)
        res = sb("res", [P, 4, D], F32, att)
        att.close()

        ps_s = ctx.enter_context(nc.psum_tensor("ps_s", [P, 4, 512], F32))
        ps_t = ctx.enter_context(nc.psum_tensor("ps_t", [P, 2, 512], F32))
        ps_o = ctx.enter_context(nc.psum_tensor("ps_o", [P, 512], F32))
        ps_m = ctx.enter_context(nc.psum_tensor("ps_m", [P, 512], F32))

        weights_in = sem("weights_in")
        biases_in = sem("biases_in")
        consts_ready = sem("consts_ready")
        pool_step = sem("pool_step")
        dve_step = sem("dve_step")
        weights_turned = sem("weights_turned")
        weights_split = sem("weights_split")
        x_in = [sem(f"x_in{s}") for s in range(RI)]
        xn_out = [sem(f"xn_out{s}") for s in range(4)]
        var_ready = sem("var_ready")
        root_ready = sem("root_ready")
        norm_ready = sem("norm_ready")
        xn_made = sem("xn_made")
        turned = sem("turned")
        hi_made = sem("hi_made")
        lo_made = sem("lo_made")
        projected = sem("projected")
        proj_kept = sem("proj_kept")
        w_in = [sem(f"w_in{s}") for s in range(RW)]
        w_hi_made = sem("w_hi_made")
        w_lo_made = sem("w_lo_made")
        bias_e_in = sem("bias_e_in")
        mask_ready = sem("mask_ready")
        counted = sem("counted")
        experts_known = sem("experts_known")
        hot_ready = sem("hot_ready")
        hot_used = sem("hot_used")
        tokens_found = sem("tokens_found")
        gather_ready = sem("gather_ready")
        rows_in = [sem(f"rows_in{s}") for s in range(RI)]
        rows_turned = sem("rows_turned")
        rows_hi = sem("rows_hi")
        rows_lo = sem("rows_lo")
        y_made = sem("y_made")
        y_biased = sem("y_biased")
        y_done = sem("y_done")
        y_out = [sem(f"y_out{s}") for s in range(4)]
        heads_zero = sem("heads_zero")
        qk_laid = sem("qk_laid")
        v_laid = sem("v_laid")
        misc_filled = sem("misc_filled")
        misc_freed = sem("misc_freed")
        heads_in = [sem(f"heads_in{s}") for s in range(3)]
        scores_ready = sem("scores_ready")
        max_done = sem("max_done")
        max_laid = sem("max_laid")
        logits_ready = sem("logits_ready")
        exp_done = sem("exp_done")
        pv_done = sem("pv_done")
        o_kept = sem("o_kept")
        o_laid = sem("o_laid")
        acc_in = [sem(f"acc_in{s}") for s in range(RA)]
        ya_in = [sem(f"ya_in{s}") for s in range(RA)]
        yb_in = [sem(f"yb_in{s}") for s in range(RA)]
        y_relu = sem("y_relu")
        half_bias = sem("half_bias")
        res_out = [sem(f"res_out{s}") for s in range(4)]

        misc = []

        def misc_plan(b, u):
            plan = {0: ([], [("o", b - 1, 1)]),
                    1: ([("max", b, 1)], [("k", b + 2, 0)]),
                    2: ([("turn", b - 1, 0)], [("k", b + 2, 1)]),
                    3: ([("out", b - 1, 0)], [("q", b + 2, 0)]),
                    4: ([("out", b - 1, 1)], [("q", b + 2, 1)]),
                    5: ([("out", b - 1, 2)], []),
                    6: ([("out", b - 1, 3)], [("o", b, 0)]),
                    7: ([("max", b + 1, 0)], [])}[u]
            return [[j for j in half if 0 <= j[1] < B] for half in plan]

        FIRST = [("k", 0, 0), ("k", 0, 1), ("q", 0, 0), ("q", 0, 1)]
        SECOND = [("k", 1, 0), ("k", 1, 1), ("q", 1, 0), ("q", 1, 1), ("max", 0, 0)]
        LAST = [("o", B - 1, 1), ("turn", B - 1, 0)] + [("out", B - 1, i) for i in range(QT)]
        misc += FIRST + SECOND
        for b in range(B):
            for u in range(2 * HG):
                for half in misc_plan(b, u):
                    misc += half
        misc += LAST
        misc_no = {job: n for n, job in enumerate(misc)}

        def result_made(i):
            return misc_no[("out", i // QT, i % QT)] + 1

        block = ctx.enter_context(nc.Block())

        @block.sync
        def _(sp):
            sp.dma_start(row_mid[:, 0, :], wqk).then_inc(weights_in, 16)
            sp.dma_start(row_mid[0:HD, 1, :], wv).then_inc(weights_in, 16)
            wo_src = wo.rearrange("(c p) k -> p c k", p=P)
            wo_dst = row_mid[:, 2, :].rearrange("p (c k) -> p c k", c=KC)
            sp.dma_start(wo_dst[:, :, 0:HD], wo_src).then_inc(weights_in, 16)
            sp.dma_start(wo_dst[:, :, HD:2 * HD], wo_src).then_inc(weights_in, 16)
            sp.dma_start(gate_w[:], wg.rearrange("(c p) e -> p c e", p=P)).then_inc(weights_in, 16)

            def load_x(i):
                if i >= RI:
                    sp.wait_ge(xn_made, i - RI + 1)
                sp.dma_start(row_in[:, i % RI, :], x_rows[i * P:(i + 1) * P, :]).then_inc(x_in[i % RI], 16)

            def load_w(c):
                if c >= RW:
                    sp.wait_ge(w_lo_made, c - RW + 1)
                e, half = divmod(c, 2)
                src = we[e].rearrange("(c p) h -> p c h", p=P)[:, 2 * half:2 * half + 2, :]
                sp.dma_start(stage[:, c % RW, :, :], src).then_inc(w_in[c % RW], 16)

            for i in range(RI):
                load_x(i)

            def row(ap):
                return ap.rearrange("(a d) -> a d", a=1).to_broadcast([P, ap.shape[0]])

            sp.dma_start(bias_p[:, 0:2 * HD], row(bqk)).then_inc(biases_in, 16)
            sp.dma_start(bias_p[:, 2 * HD:3 * HD], row(bv)).then_inc(biases_in, 16)
            sp.dma_start(bias_p[:, 3 * HD:PW], row(bg)).then_inc(biases_in, 16)
            sp.dma_start(bias_o[:], row(bo)).then_inc(biases_in, 16)
            for c in range(RW):
                load_w(c)
            for i in range(NT):
                sp.wait_ge(xn_made, i + 1)
                sp.dma_start(xn_dram[i * P:(i + 1) * P, :], row_mid[:, i % 4, :]).then_inc(xn_out[i % 4], 16)
                if i + RI < NT:
                    load_x(i + RI)
                if RW <= i + RW - 2 < NT:
                    load_w(i + RW - 2)
            sp.wait_ge(projected, NT)
            sp.wait_ge(w_lo_made, 2 * NE)
            sp.wait_ge(w_hi_made, 2 * NE)
            sp.dma_start(bias_e[:], be.rearrange("(a e) h -> a e h", a=1).to_broadcast([P, NE, F])).then_inc(bias_e_in, 16)

            for n in range(NS):
                sp.wait_ge(y_done, n + 1)
                sp.dma_start(y_dram[n * P:(n + 1) * P, :], row_mid[:, n % 4, :]).then_inc(y_out[n % 4], 16)

            def load_acc(i):
                if i >= RA:
                    sp.wait_ge(misc_freed, result_made(i - RA))
                sp.dma_start(acc[:, i % RA, :], x_rows[i * P:(i + 1) * P, :]).then_inc(acc_in[i % RA], 16)

            def load_heads(b, g):
                sp.wait_ge(misc_freed, misc_no[("k", b, g)] + 1)
                if b == 0 and g == 0:
                    sp.wait_ge(heads_zero, 3)
                if b >= 3:
                    sp.wait_ge(logits_ready, (b - 2) * 2 * HG * HG)
                for j in range(HG):
                    rows = slice(32 * j, 32 * j + 32)
                    sp.dma_start(k_head[rows, b % 3, g * HG + j, :].bitcast(F32), k_t[rows, b % 2, g, :].bitcast(F32)).then_inc(heads_in[b % 3], 16)

            sp.wait_ge(y_biased, NS)
            sp.wait_ge(y_done, NS)
            sp.wait_ge(y_made, NS)
            for i in range(RA):
                load_acc(i)
            for b in range(2):
                for g in range(G):
                    load_heads(b, g)
            for b in range(2, B + 2):
                if b < B:
                    for g in range(G):
                        load_heads(b, g)
                if b >= 3:
                    for i in range(QT * (b - 3), QT * (b - 2)):
                        sp.wait_ge(misc_freed, result_made(i))
                        sp.dma_start(out_rows[i * P:(i + 1) * P, :], res[:, i % 4, :]).then_inc(res_out[i % 4], 16)
                        if i + RA < NT:
                            load_acc(i + RA)
            for i in range(QT * (B - 1), NT):
                sp.wait_ge(misc_freed, result_made(i))
                sp.dma_start(out_rows[i * P:(i + 1) * P, :], res[:, i % 4, :]).then_inc(res_out[i % 4], 16)
            for s in range(4):
                sp.wait_ge(res_out[s], 16 * NT // 4)

        @block.gpsimd
        def _(pool):
            steps = [0]

            def link(ins):
                steps[0] += 1
                ins.then_inc(pool_step, 1)
                pool.wait_ge(pool_step, steps[0])

            link(pool.memset(ident[:], 0.0))
            pool.affine_select(out=ident[:], in_=ident[:], compare_op=ALU.not_equal, fill=1.0, base=0,
                               pattern=[[-1, P]], channel_multiplier=1).then_inc(consts_ready, 1)
            pool.memset(eps_t[:], EPS).then_inc(consts_ready, 1)
            link(pool.memset(ones[:], 1.0))
            pool.affine_select(out=before[:], in_=ones[:], compare_op=ALU.is_gt, fill=0.0, base=0,
                               pattern=[[1, P]], channel_multiplier=-1).then_inc(consts_ready, 1)
            link(pool.iota(ramp_i[:], pattern=[[1, P]], base=0, channel_multiplier=0))
            pool.tensor_copy(ramp[:], ramp_i[:]).then_inc(consts_ready, 1)
            link(pool.iota(part_i[:], pattern=[[0, 1]], base=0, channel_multiplier=1))
            pool.tensor_copy(part[:], part_i[:]).then_inc(consts_ready, 1)
            link(pool.memset(lower[:], 1.0))
            pool.affine_select(out=lower[:], in_=lower[:], compare_op=ALU.is_gt, fill=0.0, base=0,
                               pattern=[[1, NE], [-1, NE]], channel_multiplier=0).then_inc(consts_ready, 1)

            for c in range(2 * NE):
                e, half = divmod(c, 2)
                pool.wait_ge(w_in[c % RW], 16 * (c // RW + 1))
                pool.wait_ge(w_hi_made, c + 1)
                cs = slice(2 * half, 2 * half + 2)
                pool.tensor_tensor(w_lo[:, e, cs, :], stage[:, c % RW, :, :], w_hi[:, e, cs, :].bitcast(F32),
                                   ALU.subtract).then_inc(w_lo_made, 1)

            for s in range(4):
                pool.wait_ge(xn_out[s], 16 * NT // 4)
            pool.wait_ge(xn_made, NT)
            pool.wait_ge(gather_ready, 1)

            def gather(n):
                if n >= RI:
                    pool.wait_ge(rows_turned, n - RI + 1)
                pool.indirect_dma_start(row_in[:, n % RI, :], None, xn_dram,
                                        bass.IndirectOffsetOnAxis(ap=gather_i[:, n:n + 1], axis=0)).then_inc(rows_in[n % RI], 16)

            for n in range(RI):
                gather(n)
            pool.wait_ge(biases_in, 64)
            pool.tensor_scalar(bias_o[:], bias_o[:], 0.5, None, ALU.mult).then_inc(half_bias, 1)
            pool.wait_ge(half_bias, 1)
            for n in range(NS):
                pool.wait_ge(y_relu, n + 1)
                pool.tensor_tensor(row_mid[:, n % 4, :], row_mid[:, n % 4, :], bias_o[:], ALU.add).then_inc(y_done, 1)
                if n + RI < NS:
                    gather(n + RI)

            pool.wait_ge(y_made, NS)
            pool.wait_ge(y_biased, NS)
            pool.memset(k_head[:, 1, :, :].bitcast(F32), 0.0).then_inc(heads_zero, 1)
            pool.memset(k_head[:, 2, :, :].bitcast(F32), 0.0).then_inc(heads_zero, 1)
            for s in range(4):
                pool.wait_ge(y_out[s], 16 * ((NS - s + 3) // 4))

            def add_rows(i, r, before_it, landed):
                pool.wait_ge(before_it[i % RA], 16 * (i // RA + 1))
                pool.indirect_dma_start(acc[:, i % RA, :], None, y_dram,
                                        bass.IndirectOffsetOnAxis(ap=slots_i[:, r, i:i + 1], axis=0),
                                        compute_op=ALU.add).then_inc(landed[i % RA], 16)

            for i in range(NT + 2):
                if i < NT:
                    add_rows(i, 0, acc_in, ya_in)
                if i >= 2:
                    add_rows(i - 2, 1, ya_in, yb_in)

        @block.scalar
        def _(act):
            act.wait_ge(consts_ready, 2)
            act.wait_ge(weights_turned, 1)
            act.activation(wo_hi[:], ps_m[:], ACT.Copy).then_inc(weights_split, 1)

            def split_w(c):
                e, half = divmod(c, 2)
                act.wait_ge(w_in[c % RW], 16 * (c // RW + 1))
                act.activation(w_hi[:, e, 2 * half:2 * half + 2, :], stage[:, c % RW, :, :],
                               ACT.Copy).then_inc(w_hi_made, 1)

            def hi(i):
                act.wait_ge(turned, i + 1)
                if i >= 2:
                    act.wait_ge(projected, i - 1)
                act.activation(t_hi[:, i % 2, :], ps_t[:, i % 2, :], ACT.Copy).then_inc(hi_made, 1)

            def root(g):
                act.wait_ge(var_ready, g + 1)
                act.activation(small[:, 1, 2 * g:2 * g + 2], small[:, 0, 2 * g:2 * g + 2], ACT.Sqrt).then_inc(root_ready, 1)

            root(0)
            for i in range(NT):
                act.wait_ge(norm_ready, i // 2 + 1)
                act.wait_ge(x_in[i % RI], 16 * (i // RI + 1))
                if i == 0:
                    act.wait_ge(weights_turned, 2)
                if i >= 4:
                    act.wait_ge(turned, i - 3)
                    act.wait_ge(xn_out[i % 4], 16 * (i // 4))
                act.activation(row_mid[:, i % 4, :], row_in[:, i % RI, :], ACT.Identity,
                               bias=small[:, 6, i:i + 1], scale=small[:, 5, i:i + 1]).then_inc(xn_made, 1)
                if i >= 1:
                    hi(i - 1)
                if i % 2 == 0 and i + 2 < NT:
                    root(i // 2 + 1)
                split_w(i)
            hi(NT - 1)

            def rows_high(n):
                act.wait_ge(rows_turned, n + 1)
                if n >= 2:
                    act.wait_ge(y_made, n - 1)
                act.activation(t_hi[:, n % 2, :], ps_t[:, n % 2, :], ACT.Copy).then_inc(rows_hi, 1)

            for n in range(NS):
                rows_high(n)
                if n >= 1:
                    act.wait_ge(y_biased, n)
                    act.activation(row_mid[:, (n - 1) % 4, :], row_mid[:, (n - 1) % 4, :], ACT.Relu,
                                   scale=0.5).then_inc(y_relu, 1)
            act.wait_ge(y_biased, NS)
            act.activation(row_mid[:, (NS - 1) % 4, :], row_mid[:, (NS - 1) % 4, :], ACT.Relu,
                           scale=0.5).then_inc(y_relu, 1)

            def keep(kind, b, g):
                m = misc_no[(kind, b, g)]
                act.wait_ge(misc_filled, m + 1)
                if kind == "k":
                    if b >= 2:
                        act.wait_ge(heads_in[(b - 2) % 3], 16 * H * ((b - 2) // 3 + 1))
                    dst = k_t[:, b % 2, g, :]
                elif kind == "q":
                    if b >= 2:
                        act.wait_ge(misc_freed, misc_no[("max", b - 2, G - 1)] + 1)
                        act.wait_ge(scores_ready, (b - 1) * 2 * H)
                    dst = q_t[:, b % 2, g, :]
                else:
                    if b >= 1:
                        act.wait_ge(misc_filled, misc_no[("out", b - 1, QT - 1)] + 1)
                    dst = o_t[:]
                act.activation(dst, ps_m[:], ACT.Copy).then_inc(misc_freed, 1)

            for job in FIRST + SECOND[:-1]:
                keep(*job)

            def keep_o(b, g):
                act.wait_ge(pv_done, 2 * HG * b + HG * (g + 1))
                if 2 * b + g >= 2:
                    act.wait_ge(misc_filled, misc_no[("o", b - 1, g)] + 1)
                act.activation(o_sum[:, g, :], ps_o[:], ACT.Copy).then_inc(o_kept, 1)

            for b in range(B):
                for u in range(2 * HG):
                    n = 2 * HG * b + u
                    mid, end = misc_plan(b, u)
                    for j in range(HG):
                        act.wait_ge(logits_ready, HG * n + j + 1)
                        if j == 0 and n >= 2:
                            act.wait_ge(pv_done, n - 1)
                        act.activation(probs[:, n % 2, j, :], ps_t[:, j % 2, :], ACT.Exp).then_inc(exp_done, 1)
                        if j == 1:
                            if u == 0 and b >= 1:
                                keep_o(b - 1, 1)
                            if u == HG:
                                keep_o(b, 0)
                            for job in mid:
                                if job[0] in ("k", "q", "turn"):
                                    keep(*job)
                    for job in end:
                        if job[0] in ("k", "q", "turn"):
                            keep(*job)
            keep_o(B - 1, 1)
            keep("turn", B - 1, 0)

        @block.vector
        def _(dve):
            steps = [0]

            def link(ins):
                steps[0] += 1
                ins.then_inc(dve_step, 1)
                dve.wait_ge(dve_step, steps[0])

            dve.memset(ps_o[:], 0.0).then_inc(dve_step, 1)
            steps[0] += 1
            dve.wait_ge(weights_turned, 1)
            dve.wait_ge(weights_split, 1)
            dve.tensor_tensor(wo_lo[:], ps_m[:], wo_hi[:].bitcast(F32), ALU.subtract).then_inc(weights_split, 1)
            dve.wait_ge(weights_turned, 2)
            dve.wait_ge(weights_in, 80)
            wp_ps = ps_s[:, 2:4, :].rearrange("p a (c n) -> p (a c) n", c=2)
            link(dve.tensor_copy(wp_hi[:, :, 0:3 * HD], wp_ps[:, :, 0:3 * HD]))
            link(dve.tensor_copy(wp_hi[:, :, 3 * HD:PW], gate_w[:]))
            dve.tensor_tensor(wp_lo[:, :, 0:3 * HD], wp_ps[:, :, 0:3 * HD], wp_hi[:, :, 0:3 * HD].bitcast(F32),
                              ALU.subtract).then_inc(weights_split, 1)
            dve.tensor_tensor(wp_lo[:, :, 3 * HD:PW], gate_w[:], wp_hi[:, :, 3 * HD:PW].bitcast(F32),
                              ALU.subtract).then_inc(weights_split, 1)

            def moments(g):
                for i in (2 * g, 2 * g + 1):
                    dve.wait_ge(x_in[i % RI], 16 * (i // RI + 1))
                    dve.bn_stats(stats[:, g % 2, i % 2, :], row_in[:, i % RI, :]).then_inc(dve_step, 1)
                    steps[0] += 1
                for i in (2 * g, 2 * g + 1):
                    dve.wait_ge(dve_step, steps[0] - 1 + i % 2 if i % 2 else steps[0] - 1)
                    dve.bn_aggr(mv[:, i, :], stats[:, g % 2, i % 2, :]).then_inc(dve_step, 1)
                    steps[0] += 1
                dve.wait_ge(dve_step, steps[0])
                ts = slice(2 * g, 2 * g + 2)
                dve.tensor_scalar(small[:, 0, ts], mv[:, ts, 1], EPS, None, ALU.add).then_inc(var_ready, 1)

            def scales(g):
                ts = slice(2 * g, 2 * g + 2)
                d, r, a, c = (small[:, k, ts] for k in (0, 2, 3, 4))
                dve.wait_ge(var_ready, g + 1)
                dve.wait_ge(root_ready, g + 1)
                link(dve.reciprocal(r, small[:, 1, ts]))
                link(dve.tensor_tensor(a, r, r, ALU.mult))
                link(dve.tensor_tensor(c, a, d, ALU.mult))
                link(dve.tensor_scalar(a, c, -0.5, 1.5, ALU.mult, ALU.add))
                link(dve.tensor_tensor(small[:, 5, ts], r, a, ALU.mult))
                dve.scalar_tensor_tensor(out=small[:, 6, ts], in0=mv[:, ts, 0], scalar=-1.0,
                                         in1=small[:, 5, ts], op0=ALU.mult, op1=ALU.mult).then_inc(norm_ready, 1)

            def low(i):
                dve.wait_ge(hi_made, i + 1)
                if i >= 2:
                    dve.wait_ge(projected, i - 1)
                dve.tensor_tensor(t_lo[:, i % 2, :], ps_t[:, i % 2, :], t_hi[:, i % 2, :].bitcast(F32),
                                  ALU.subtract).then_inc(lo_made, 1)

            def keep_proj(i):
                dve.wait_ge(projected, i + 1)
                if i == 0:
                    dve.wait_ge(biases_in, 64)
                dve.tensor_tensor(proj[:, i, :], ps_s[:, i % 2, 0:PW], bias_p[:], ALU.add).then_inc(proj_kept, 1)

            def top(i):
                dve.wait_ge(proj_kept, i + 1)
                logits = proj[:, i, 3 * HD:PW]
                link(dve.max(top_v[:, i, :], logits))
                dve.max_index(top_i[:, i, :], top_v[:, i, :], logits).then_inc(dve_step, 1)
                steps[0] += 1

            moments(0)
            moments(1)
            scales(0)
            for i in range(NT):
                if i % 2 == 1 and i + 1 < NT:
                    scales(i // 2 + 1)
                low(i)
                if i >= 1:
                    keep_proj(i - 1)
                if i % 2 == 0 and i + 4 < NT:
                    moments(i // 2 + 2)
                if i >= 1:
                    top(i - 1)
            keep_proj(NT - 1)
            top(NT - 1)

            dve.wait_ge(dve_step, steps[0])
            link(dve.tensor_copy(top_f[:], top_i[:]))
            dve.wait_ge(consts_ready, 6)
            ramp8 = ramp[:, 0:NE].unsqueeze(1).to_broadcast([P, NT, NE])
            for r in range(2):
                ins = dve.tensor_tensor(pick[:, r], ramp8, top_f[:, :, r:r + 1].to_broadcast([P, NT, NE]), ALU.is_equal)
                ins.then_inc(dve_step, 1)
                steps[0] += 1
            dve.memset(mask[:, NT, :], 0.0).then_inc(mask_ready, 1)
            dve.wait_ge(dve_step, steps[0])
            dve.tensor_tensor(mask[:, 0:NT, :], pick[:, 0], pick[:, 1], ALU.add).then_inc(mask_ready, 1)

            dve.wait_ge(counted, 1)
            ps_c = ps_m[:, 0:(NT + 1) * NE].rearrange("p (i e) -> p i e", e=NE)
            link(dve.tensor_copy(place[:], ps_c))
            thresholds = ramp[:, 0:NT].unsqueeze(1).to_broadcast([P, NE, NT])
            counts = ecol[:, 0, :]
            link(dve.tensor_scalar(counts, place[:, NT, :], 1.0 / P, None, ALU.mult))
            link(dve.tensor_tensor(tiles_gt[:], counts.unsqueeze(2).to_broadcast([P, NE, NT]), thresholds, ALU.is_gt))
            link(dve.tensor_reduce(ecol[:, 1, :], tiles_gt[:], AX.X, ALU.add))
            link(dve.tensor_tensor(tri[:], lower[:], ecol[:, 1:2, :].to_broadcast([P, NE, NE]), ALU.mult))
            link(dve.tensor_reduce(ecol[:, 2, :], tri[:], AX.X, ALU.add))
            link(dve.tensor_tensor(ecol[:, 3, :], ecol[:, 1, :], ecol[:, 2, :], ALU.add))
            link(dve.tensor_scalar(ecol[:, 0, :], ecol[:, 2, :], float(P), None, ALU.mult))
            link(dve.tensor_tensor(place[:, 0:NT, :], place[:, 0:NT, :], ecol[:, 0:1, :].to_broadcast([P, NT, NE]), ALU.add))
            for r in range(2):
                link(dve.tensor_tensor(slot_p[:, r], place[:, 0:NT, :], pick[:, r], ALU.mult))
            link(dve.tensor_reduce(slot_f[:], slot_p[:], AX.X, ALU.add))
            link(dve.tensor_copy(slots_i[:], slot_f[:]))
            link(dve.tensor_scalar(slot_r[:, 0], slots_i[:], P - 1, None, ALU.bitwise_and))
            link(dve.tensor_scalar(slot_r[:, 1], slots_i[:], P.bit_length() - 1, None, ALU.arith_shift_right))
            link(dve.tensor_copy(slot_q[:], slot_r[:].rearrange("p a r i -> p a (r i)")))
            ramp_s = ramp[:, 0:NS].unsqueeze(1).to_broadcast([P, NC, NS])
            link(dve.tensor_tensor(hot_tile[:], ramp_s, slot_q[:, 1, :].unsqueeze(2).to_broadcast([P, NC, NS]), ALU.is_equal))
            for r in range(2):
                tile_no = ramp[:, 0:NT].unsqueeze(2).to_broadcast([P, NT, NS])
                cs = slice(r * NT, (r + 1) * NT)
                dve.tensor_tensor(hot_val[:, cs, 0, :], hot_tile[:, cs, :], tile_no, ALU.mult).then_inc(hot_ready, 1)
            dve.tensor_scalar(hot_val[:, :, 1, :], hot_tile[:], part[:, 0:1], None, ALU.mult).then_inc(hot_ready, 1)
            for c in range(NC // 4):
                if c >= 2:
                    dve.wait_ge(hot_used, c - 1)
                ramp_r = ramp[:].unsqueeze(1).to_broadcast([P, 4, P])
                slot_row = slot_q[:, 0, 4 * c:4 * c + 4].unsqueeze(2).to_broadcast([P, 4, P])
                dve.tensor_tensor(hot_row[:, c % 2], ramp_r, slot_row, ALU.is_equal).then_inc(hot_ready, 1)
            link(dve.tensor_tensor(te_cmp[:], ecol[:, 3:4, :].to_broadcast([P, NS, NE]),
                                   ramp[:, 0:NS].unsqueeze(2).to_broadcast([P, NS, NE]), ALU.is_le))
            link(dve.tensor_reduce(te_f[:], te_cmp[:], AX.X, ALU.add))
            dve.tensor_scalar(expert_i[:], te_f[:], float(NE - 1), None, ALU.min).then_inc(experts_known, 1)
            dve.wait_ge(tokens_found, 1)
            found = ps_s[:, 3, 0:2 * NS].rearrange("p (a n) -> p a n", a=2)
            link(dve.tensor_copy(tok_f[:], found))
            dve.scalar_tensor_tensor(out=gather_i[:], in0=tok_f[:, 0, :], scalar=float(P), in1=tok_f[:, 1, :],
                                     op0=ALU.mult, op1=ALU.add).then_inc(gather_ready, 1)

            def rows_low(n):
                dve.wait_ge(rows_hi, n + 1)
                dve.tensor_tensor(t_lo[:, n % 2, :], ps_t[:, n % 2, :], t_hi[:, n % 2, :].bitcast(F32),
                                  ALU.subtract).then_inc(rows_lo, 1)

            dve.wait_ge(experts_known, 1)
            dve.wait_ge(bias_e_in, 16)
            for n in range(NS + 1):
                if n < NS:
                    rows_low(n)
                if n >= 1:
                    e = dve.value_load(expert_i[0:1, n - 1:n], min_val=0, max_val=NE - 1)
                    dve.wait_ge(y_made, n)
                    if n > 4:
                        dve.wait_ge(y_out[(n - 1) % 4], 16 * ((n - 1) // 4))
                    dve.tensor_tensor(row_mid[:, (n - 1) % 4, :], ps_s[:, (n - 1) % 2, :], bias_e[:, bass.ds(e, 1), :].rearrange("p a h -> p (a h)"),
                                      ALU.add).then_inc(y_biased, 1)

            dve.wait_ge(y_biased, NS)
            dve.memset(k_head[:, 0, :, :].bitcast(F32), 0.0).then_inc(heads_zero, 1)
            link(dve.memset(a_q[:], 0.0))
            link(dve.memset(a_k[:], 0.0))
            link(dve.memset(a_m[:], 0.0))
            heads_q = a_q[:].rearrange("p i (h c) -> p i h c", c=32)
            heads_k = a_k[:].rearrange("p i (h c) -> p i h c", c=32)
            heads_m = a_m[:].rearrange("p i (h c) -> p i h c", c=32)
            link(dve.memset(heads_k[:, :, :, 0:2], 1.0))
            link(dve.memset(v_ones[:, :, :, HE:VC], float(HD) ** 0.5))
            dve.wait_ge(dve_step, steps[0])

            def lay_qk(b):
                src = proj[:, QT * b:QT * (b + 1), 0:2 * HD].rearrange("p i (h e s) -> p i h e s", e=HE, s=2)
                if b >= 1:
                    dve.wait_ge(misc_filled, misc_no[("q", b - 1, G - 1)] + 1)
                for s, heads, hi_at, lo_at in ((0, heads_q, (2, 10), 18), (1, heads_k, (2, 18), 10)):
                    exact = src[:, :, :, :, s]
                    hi = heads[:, :, :, hi_at[0]:hi_at[0] + HE]
                    for i in range(QT):
                        dve.tensor_copy(hi[:, i].bitcast(F32R), exact[:, i]).then_inc(dve_step, 1)
                        dve.tensor_copy(heads[:, i, :, hi_at[1]:hi_at[1] + HE].bitcast(F32R), exact[:, i]).then_inc(dve_step, 1)
                        steps[0] += 2
                    dve.wait_ge(dve_step, steps[0])
                    for i in range(QT):
                        dve.tensor_tensor(heads[:, i, :, lo_at:lo_at + HE], exact[:, i], hi[:, i], ALU.subtract).then_inc(qk_laid, 1)
                dve.tensor_copy(v_ones[:, QT * b:QT * (b + 1), :, 0:HE],
                                proj[:, QT * b:QT * (b + 1), 2 * HD:3 * HD].rearrange("p i (h e) -> p i h e", e=HE)).then_inc(v_laid, 1)

            def maxima(b, h):
                for half in range(2):
                    n = 2 * (H * b + h) + half
                    dve.wait_ge(scores_ready, n + 1)
                    if b >= 2 and h == 0 and half == 0:
                        dve.wait_ge(max_laid, 2 * (b - 1))
                    dve.tensor_reduce(row_max[:, b % 2, h, 2 * half:2 * half + 2], ps_s[:, 2 * half:2 * half + 2, :],
                                      AX.X, ALU.max).then_inc(max_done, 1)

            def lay_max(b, g):
                dve.wait_ge(max_done, 2 * H * b + 2 * HG * (g + 1))
                if b >= 1:
                    dve.wait_ge(misc_filled, misc_no[("max", b - 1, g)] + 1)
                mx = row_max[:, b % 2, HG * g:HG * (g + 1), :].rearrange("p h i -> p i h")
                hs = slice(HG * g, HG * (g + 1))
                link(dve.tensor_scalar(heads_m[:, :, hs, 0].bitcast(F32R), mx, -1.0, None, ALU.mult))
                dve.scalar_tensor_tensor(out=heads_m[:, :, hs, 1], in0=mx, scalar=-1.0, in1=heads_m[:, :, hs, 0],
                                         op0=ALU.mult, op1=ALU.subtract).then_inc(max_laid, 1)

            def add_max(b, g):
                m = misc_no[("max", b, g)]
                dve.wait_ge(misc_filled, m + 1)
                if b >= 1:
                    dve.wait_ge(logits_ready, HG * (2 * HG * (b - 1) + HG * (g + 1)))
                dve.wait_ge(misc_freed, misc_no[("q", b, g)] + 1)
                dve.tensor_tensor(q_m[:, g, :], ps_m[:], q_t[:, b % 2, g, :].bitcast(F32), ALU.add).then_inc(misc_freed, 1)

            def lay_o(b, g):
                m = misc_no[("o", b, g)]
                dve.wait_ge(misc_filled, m + 1)
                sums = ps_m[:].rearrange("p (i j c) -> p i j c", j=HG, c=32)
                if b >= 1 and g == 0:
                    dve.wait_ge(misc_filled, misc_no[("turn", b - 1, 0)] + 1)
                link(dve.reciprocal(o_inv[:], sums[:, :, :, HE]))
                cs = slice(g * HG * HE, (g + 1) * HG * HE)
                exact = o_exact[:, :, cs].rearrange("p i (j e) -> p i j e", e=HE)
                steps[0] += 1
                for i in range(QT):
                    ins = dve.tensor_tensor(exact[:, i], sums[:, i, :, 0:HE], o_inv[:, i, :].unsqueeze(2).to_broadcast([P, HG, HE]), ALU.mult)
                    if i < QT - 1:
                        ins.then_inc(dve_step, 1)
                        steps[0] += 1
                steps[0] -= 1
                ins.then_inc(misc_freed, 1)
                dve.wait_ge(dve_step, steps[0])
                dve.wait_ge(misc_freed, m + 1)
                link(dve.tensor_copy(o_tok[:, :, cs].bitcast(F32R), o_exact[:, :, cs]))
                dve.tensor_tensor(o_tok[:, :, HD + g * HG * HE:HD + (g + 1) * HG * HE], o_exact[:, :, cs],
                                  o_tok[:, :, cs], ALU.subtract).then_inc(o_laid, 1)

            def result(b, i):
                n = QT * b + i
                m = misc_no[("out", b, i)]
                dve.wait_ge(yb_in[n % RA], 16 * (n // RA + 1))
                if n >= 4:
                    dve.wait_ge(res_out[n % 4], 16 * (n // 4))
                dve.wait_ge(misc_filled, m + 1)
                dve.tensor_tensor(res[:, n % 4, :], ps_m[:], acc[:, n % RA, :], ALU.add).then_inc(misc_freed, 1)

            def serve(jobs):
                for kind, b, g in jobs:
                    if kind == "max":
                        add_max(b, g)
                    elif kind == "o":
                        lay_o(b, g)
                    elif kind == "out":
                        result(b, g)

            lay_qk(0)
            lay_qk(1)
            for h in range(H):
                maxima(0, h)
            lay_max(0, 0)
            add_max(0, 0)
            lay_max(0, 1)
            for b in range(B):
                for u in range(2 * HG):
                    mid, end = misc_plan(b, u)
                    if u == 0 and b + 2 < B:
                        lay_qk(b + 2)
                    if b + 1 < B:
                        maxima(b + 1, u)
                    if u == 3 and b + 1 < B:
                        lay_max(b + 1, 0)
                    if u == 7 and b + 1 < B:
                        lay_max(b + 1, 1)
                    serve(mid)
                    serve(end)
            serve(LAST)

        @block.tensor
        def _(pe):
            pe.wait_ge(consts_ready, 1)
            pe.wait_ge(weights_in, 80)
            for c in range(KC):
                mm = pe.transpose(ps_m[:, c * P:(c + 1) * P], row_mid[:, 2, c * P:(c + 1) * P], ident[:])
            mm.then_inc(weights_turned, 1)
            wp_ps = ps_s[:, 2:4, :].rearrange("p a (c n) -> p (a c) n", c=2)
            for c in range(KC):
                pe.transpose(wp_ps[:, c, 0:P], row_mid[:, 0, c * P:(c + 1) * P], ident[:])
                mm = pe.transpose(wp_ps[:, c, P:P + HD], row_mid[0:HD, 1, c * P:(c + 1) * P], ident[0:HD, 0:HD])
            mm.then_inc(weights_turned, 1)

            def turn(i):
                pe.wait_ge(xn_made, i + 1)
                if i >= 2:
                    pe.wait_ge(lo_made, i - 1)
                for c in range(KC):
                    mm = pe.transpose(ps_t[:, i % 2, c * P:(c + 1) * P], row_mid[:, i % 4, c * P:(c + 1) * P], ident[:])
                mm.then_inc(turned, 1)

            def project(i):
                pe.wait_ge(hi_made, i + 1)
                pe.wait_ge(lo_made, i + 1)
                if i == 0:
                    pe.wait_ge(weights_split, 4)
                if i >= 2:
                    pe.wait_ge(proj_kept, i - 1)
                n = 0
                for c in range(KC):
                    ks = slice(c * P, (c + 1) * P)
                    for a, w in ((t_hi, wp_hi), (t_hi, wp_lo), (t_lo, wp_hi)):
                        mm = pe.matmul(ps_s[:, i % 2, 0:PW], a[:, i % 2, ks], w[:, c, :], start=(n == 0), stop=(n == 3 * KC - 1))
                        n += 1
                mm.then_inc(projected, 1)

            for i in range(NT):
                turn(i)
                if i >= 1:
                    project(i - 1)
            project(NT - 1)

            pe.wait_ge(mask_ready, 2)
            counts = ps_m[:, 0:(NT + 1) * NE].rearrange("p (i e) -> p i e", e=NE)
            pe.matmul(counts[:, :, :], before[:], mask[:, :, :], start=True, stop=False)
            for i in range(NT):
                later = NT - i
                mm = pe.matmul(counts[:, i + 1:NT + 1, :], ones[:], mask[:, i:i + 1, :].to_broadcast([P, later, NE]),
                               start=False, stop=(i == NT - 1))
            mm.then_inc(counted, 1)
            pe.wait_ge(hot_ready, 3)
            for c in range(NC):
                if c % 4 == 0:
                    pe.wait_ge(hot_ready, 4 + c // 4)
                mm = pe.matmul(ps_s[:, 3, 0:2 * NS], hot_row[:, (c // 4) % 2, c % 4, :], hot_val[:, c].rearrange("p a n -> p (a n)"),
                               start=(c == 0), stop=(c == NC - 1))
                if c % 4 == 3 and c < NC - 1:
                    mm.then_inc(hot_used, 1)
            mm.then_inc(tokens_found, 1)

            def turn_rows(n):
                pe.wait_ge(rows_in[n % RI], 16 * (n // RI + 1))
                if n >= 2:
                    pe.wait_ge(rows_lo, n - 1)
                for c in range(KC):
                    mm = pe.transpose(ps_t[:, n % 2, c * P:(c + 1) * P], row_in[:, n % RI, c * P:(c + 1) * P], ident[:])
                mm.then_inc(rows_turned, 1)

            pe.wait_ge(experts_known, 1)
            pe.wait_ge(w_hi_made, 2 * NE)
            pe.wait_ge(w_lo_made, 2 * NE)
            turn_rows(0)
            for n in range(NS):
                e = pe.value_load(expert_i[0:1, n:n + 1], min_val=0, max_val=NE - 1)
                if n + 1 < NS:
                    turn_rows(n + 1)
                pe.wait_ge(rows_hi, n + 1)
                pe.wait_ge(rows_lo, n + 1)
                if n >= 2:
                    pe.wait_ge(y_biased, n - 1)
                k = 0
                for c in range(KC):
                    ks = slice(c * P, (c + 1) * P)
                    for a, w in ((t_hi, w_hi), (t_hi, w_lo), (t_lo, w_hi)):
                        rhs = w[:, bass.ds(e, 1), c, :].rearrange("p a h -> p (a h)")
                        mm = pe.matmul(ps_s[:, n % 2, :], a[:, n % 2, ks], rhs, start=(k == 0), stop=(k == 3 * KC - 1))
                        k += 1
                mm.then_inc(y_made, 1)

            def fill(kind, b, g):
                m = misc_no[(kind, b, g)]
                if m >= 1:
                    pe.wait_ge(misc_freed, m)
                if kind in ("k", "q"):
                    pe.wait_ge(qk_laid, 2 * QT * (b + 1))
                    src = a_q if kind == "q" else a_k
                    for i in range(QT):
                        mm = pe.transpose(ps_m[:, i * P:(i + 1) * P], src[:, i, g * P:(g + 1) * P], ident[:])
                elif kind == "max":
                    pe.wait_ge(max_laid, 2 * b + g + 1)
                    for i in range(QT):
                        mm = pe.transpose(ps_m[:, i * P:(i + 1) * P], a_m[:, i, g * P:(g + 1) * P], ident[:])
                elif kind == "o":
                    pe.wait_ge(o_kept, 2 * b + g + 1)
                    for i in range(QT):
                        mm = pe.transpose(ps_m[:, i * P:(i + 1) * P], o_sum[:, g, i * P:(i + 1) * P], ident[:])
                elif kind == "turn":
                    pe.wait_ge(o_laid, 2 * b + 2)
                    for i in range(QT):
                        mm = pe.transpose(ps_m[:, i * P:(i + 1) * P], o_tok[:, i, :], ident[:])
                else:
                    pe.wait_ge(misc_freed, misc_no[("turn", b, 0)] + 1)
                    ts = slice(g * P, (g + 1) * P)
                    pe.matmul(ps_m[:], o_t[:, ts], wo_hi[:], start=True, stop=False)
                    mm = pe.matmul(ps_m[:], o_t[:, ts], wo_lo[:], start=False, stop=True)
                mm.then_inc(misc_filled, 1)

            def scores(b, h, half):
                n = 2 * (H * b + h) + half
                if half == 0 and h % HG == 0:
                    pe.wait_ge(heads_in[b % 3], 16 * H * (b // 3 + 1))
                    pe.wait_ge(misc_freed, misc_no[("q", b, h // HG)] + 1)
                if n >= 2:
                    pe.wait_ge(max_done, n - 1)
                for i in (2 * half, 2 * half + 1):
                    mm = pe.matmul(ps_s[:, i, :], q_t[:, b % 2, h // HG, i * P:(i + 1) * P], k_head[:, b % 3, h, :],
                                   start=True, stop=True)
                mm.then_inc(scores_ready, 1)

            def logits(b, u, j):
                g, kt = divmod(u, QT)
                n = HG * (2 * HG * b + u) + j
                if n >= 2:
                    pe.wait_ge(exp_done, n - 1)
                if kt == 0 and j == 0:
                    pe.wait_ge(misc_freed, misc_no[("max", b, g)] + 1)
                pe.matmul(ps_t[:, n % 2, :], k_head[:, b % 3, g * HG + j, kt * P:(kt + 1) * P], q_m[:, g, :],
                          start=True, stop=True).then_inc(logits_ready, 1)

            def values(b, u):
                g, kt = divmod(u, QT)
                n = 2 * HG * b + u
                pe.wait_ge(exp_done, HG * (n + 1))
                pe.wait_ge(v_laid, b + 1)
                if kt == 0 and n > 0:
                    pe.wait_ge(o_kept, 2 * b + g)
                for j in range(HG):
                    mm = pe.matmul(ps_o[32 * j:32 * j + VC, :], v_ones[:, QT * b + kt, g * HG + j, :], probs[:, n % 2, j, :],
                                   start=(kt == 0), stop=(kt == QT - 1))
                mm.then_inc(pv_done, 1)

            pe.wait_ge(y_biased, NS)
            for job in FIRST:
                fill(*job)
            for job in SECOND[:-1]:
                fill(*job)
            for h in range(H):
                for half in range(2):
                    scores(0, h, half)
            fill(*SECOND[-1])
            for b in range(B):
                for u in range(2 * HG):
                    mid, end = misc_plan(b, u)
                    logits(b, u, 0)
                    logits(b, u, 1)
                    if b + 1 < B:
                        scores(b + 1, u, 0)
                    if u >= 1:
                        values(b, u - 1)
                    elif b >= 1:
                        values(b - 1, 2 * HG - 1)
                    for job in mid:
                        fill(*job)
                    logits(b, u, 2)
                    logits(b, u, 3)
                    if b + 1 < B:
                        scores(b + 1, u, 1)
                    for job in end:
                        fill(*job)
            values(B - 1, 2 * HG - 1)
            for job in LAST:
                fill(*job)


_INS = ['L0_attn_x', 'L0_attn_Wqk_w', 'L0_attn_Wqk_b', 'L0_attn_Wv_w', 'L0_attn_Wv_b', 'L0_attn_Wo_w', 'L0_attn_Wo_b',
        'L0_ffn_W_gate', 'L0_ffn_b_gate', 'L0_ffn_W_e', 'L0_ffn_b_e']
_OUTS = [((B, N, D), 'float32')]


def kernel(**inputs):
    import numpy as _np
    import concourse.bacc as _bacc
    from concourse import mybir as _mybir
    from concourse.bass_utils import run_bass_kernel_spmd as _run

    nc = _bacc.Bacc("TRN2", target_bir_lowering=False, num_devices=1)
    arrays, args = {}, []
    for name in _INS:
        a = _np.ascontiguousarray(inputs[name])
        arrays[f"in_{name}_dram"] = a
        args.append(nc.dram_tensor(f"in_{name}_dram", a.shape, _mybir.dt.from_np(a.dtype), kind="ExternalInput").ap())
    for i, (shape, dtype) in enumerate(_OUTS):
        dt = _mybir.dt.from_np(_np.dtype(dtype))
        args.append(nc.dram_tensor(f"out_{i}_dram", shape, dt, kind="ExternalOutput").ap())
    attention_and_experts(nc, *args)
    r = _run(nc, [arrays], core_ids=[0])
    return r.results[0]["out_0_dram"]
```

```python
from contextlib import ExitStack

import concourse.bass as bass
from concourse import mybir

F32 = mybir.dt.float32
F32R = mybir.dt.float32r
BF16 = mybir.dt.bfloat16
I32 = mybir.dt.int32
U32 = mybir.dt.uint32
ALU = mybir.AluOpType
ACT = mybir.ActivationFunctionType
AX = mybir.AxisListType

P = 128
B, N, D = 4, 512, 512
T = B * N
NT = T // P
KC = D // P
H, HE = 8, 8
HD = H * HE
G = 2
HG = H // G
NE, F = 8, 512
PW = 3 * HD + NE
QT = N // P
NS = (2 * T + NE * (P - 1)) // P
NSE = NS + NS % 2
NC = 2 * NT
EPS = 1e-5
VC = HE + 1
RI = 6
RW = 5
RS = 3
K_LAY, Q_LAY = (0, 2, 3, 0), (0, 1, 2, 3)

FREE_0, FREE_1 = NT, 2 * NT
ZERO_AT = FREE_0 + 1
COPY_AT = ZERO_AT, ZERO_AT + 2
SCORES_AT = ZERO_AT + 4
MAX_AT = SCORES_AT + HG * QT // 2 + 1
LAY_AT = FREE_1 + 1
K_AT, Q_AT = LAY_AT + QT - 1, LAY_AT + QT
assert SCORES_AT + H * QT // 2 <= NS and Q_AT < NS - 1
LAG = 2


def attention_and_experts(nc, x, wqk, bqk, wv, bv, wo, bo, wg, bg, we, be, out):
    x_rows = x.rearrange("b n d -> (b n) d")
    out_rows = out.rearrange("b n d -> (b n) d")
    xn_dram = nc.dram_tensor("xn_rows", (T, D), F32).ap()
    y_dram = nc.dram_tensor("expert_rows", (NS * P, F), F32).ap()

    ctx = ExitStack()
    with ctx:
        def sb(name, shape, dt, where=ctx):
            return where.enter_context(nc.sbuf_tensor(name, shape, dt))

        def sem(name):
            return ctx.enter_context(nc.semaphore(name))

        ident = sb("ident", [P, P], F32)
        before = sb("before", [P, P], BF16)
        ones = sb("ones", [P, P], BF16)
        ramp_i = sb("ramp_i", [P, P], I32)
        ramp = sb("ramp", [P, P], F32)
        part_i = sb("part_i", [P, 1], I32)
        part = sb("part", [P, 1], F32)
        lower = sb("lower", [P, NE, NE], F32)
        eps_t = sb("eps_t", [P, 1], F32)
        bias_o = sb("bias_o", [P, D], F32)
        wo_hi = sb("wo_hi", [P, D], F32R)
        wo_lo = sb("wo_lo", [P, D], F32R)
        proj = sb("proj", [P, NT, PW], F32)
        slots_i = sb("slots_i", [P, 2, NT], I32)
        gather_i = sb("gather_i", [P, NS], I32)
        expert_i = sb("expert_i", [P, NS], I32)
        row_mid = sb("row_mid", [P, 4, D], F32)

        top_v = sb("top_v", [P, NT, 8], F32)
        top_i = sb("top_i", [P, NT, 8], U32)

        stats = sb("stats", [P, 2, 2, 6], F32)
        mv = sb("mv", [P, NT, 2], F32)
        small = sb("small", [P, 8, NT], F32)
        row_max = sb("row_max", [P, 2, H, QT], F32)
        rows_era = ExitStack()
        row_in = sb("row_in", [P, RI, D], F32, rows_era)
        rows_era.close()
        rout = ExitStack()
        top_f = sb("top_f", [P, NT, 8], F32, rout)
        pick = sb("pick", [P, 2, NT, NE], F32, rout)
        mask = sb("mask", [P, NT + 1, NE], BF16, rout)
        place = sb("place", [P, NT + 1, NE], F32, rout)
        tiles_gt = sb("tiles_gt", [P, NE, NT], F32, rout)
        tri = sb("tri", [P, NE, NE], F32, rout)
        ecol = sb("ecol", [P, 4, NE], F32, rout)
        te_cmp = sb("te_cmp", [P, NS, NE], F32, rout)
        te_f = sb("te_f", [P, NS], F32, rout)
        slot_p = sb("slot_p", [P, 2, NT, NE], F32, rout)
        slot_f = sb("slot_f", [P, 2, NT], F32, rout)
        slot_r = sb("slot_r", [P, 2, 2, NT], I32, rout)
        slot_q = sb("slot_q", [P, 2, NC], F32, rout)
        hot_tile = sb("hot_tile", [P, NC, NSE], F32, rout)
        token_f = sb("token_f", [P, NT], F32, rout)
        rout.close()
        sb("row_in_place", [P, RI, D], F32)
        turned_era = ExitStack()
        t_hi = sb("t_hi", [P, 2, D], F32R, turned_era)
        t_lo = sb("t_lo", [P, 2, D], F32R, turned_era)
        turned_era.close()
        hot_row = sb("hot_row", [P, 3, 4, P], F32R)
        hot_val = sb("hot_val", [P, 3, 4, NSE], F32R)
        sb("hot_gap", [P, 4 * D - 12 * P - 12 * NSE], F32)

        sub = ExitStack()
        stage = sb("stage", [P, RW, 2, F], F32, sub)
        wp_hi = sb("wp_hi", [P, KC, PW], F32R, sub)
        wp_lo = sb("wp_lo", [P, KC, PW], F32R, sub)
        gate_w = sb("gate_w", [P, KC, NE], F32, sub)
        bias_p = sb("bias_p", [P, PW], F32, sub)
        sub.close()
        lay_0 = sb("lay_0", [P, QT, G * P], F32)
        k_t0 = sb("k_t0", [P, G, N], F32R)
        q_t0 = sb("q_t0", [P, G, N], F32R)
        era = ExitStack()
        bias_e = sb("bias_e", [P, NE, F], F32, era)
        w_split = sb("w_split", [P, NE, 2, KC, F], F32R, era)
        era.close()
        k_head1 = sb("k_head1", [P, H, N], F32R)
        k_head0 = sb("k_head0", [P, H, N], F32R)
        lay_1 = sb("lay_1", [P, QT, G * P], F32)
        lay_2 = sb("lay_2", [P, QT, G * P], F32)
        k_t1 = sb("k_t1", [P, G, N], F32R)
        q_t1 = sb("q_t1", [P, G, N], F32R)
        k_head2 = sb("k_head2", [P, H, N], F32R)
        lay_3 = sb("lay_3", [P, QT, G * P], F32)
        q_t2 = sb("q_t2", [P, G, N], F32R)
        v_ones = sb("v_ones", [P, NT, H, VC], F32)
        probs = sb("probs", [P, 2, HG, N], F32)
        o_sum = sb("o_sum", [P, 2, N], F32)
        o_inv = sb("o_inv", [P, QT, HG], F32)
        o_tok = sb("o_tok", [P, QT, P], F32)
        o_exact = sb("o_exact", [P, QT, HD], F32)
        o_t = sb("o_t", [P, N], F32R)
        acc = sb("acc", [P, NT, D], F32)
        res = sb("res", [P, 4, D], F32)
        lay = [lay_0, lay_1, lay_2, lay_3]
        k_t = [k_t0, k_t1]
        q_t = [q_t0, q_t1, q_t2]
        k_head = [k_head0, k_head1, k_head2]

        ps_s = ctx.enter_context(nc.psum_tensor("ps_s", [P, RS, 512], F32))
        ps_t = ctx.enter_context(nc.psum_tensor("ps_t", [P, 2, 512], F32))
        ps_o = ctx.enter_context(nc.psum_tensor("ps_o", [P, 512], F32))
        ps_m = ctx.enter_context(nc.psum_tensor("ps_m", [P, 2, 512], F32))

        weights_in = sem("weights_in")
        biases_in = sem("biases_in")
        consts_ready = sem("consts_ready")
        pool_step = sem("pool_step")
        dve_step = sem("dve_step")
        weights_turned = sem("weights_turned")
        weights_split = sem("weights_split")
        x_in = [sem(f"x_in{s}") for s in range(RI)]
        xn_out = [sem(f"xn_out{s}") for s in range(4)]
        var_ready = sem("var_ready")
        root_ready = sem("root_ready")
        norm_ready = sem("norm_ready")
        xn_made = sem("xn_made")
        turned = sem("turned")
        hi_made = sem("hi_made")
        lo_made = sem("lo_made")
        projected = sem("projected")
        proj_kept = sem("proj_kept")
        w_in = [sem(f"w_in{s}") for s in range(RW)]
        w_hi_made = sem("w_hi_made")
        w_lo_made = sem("w_lo_made")
        bias_e_in = sem("bias_e_in")
        mask_ready = sem("mask_ready")
        counted = sem("counted")
        experts_known = sem("experts_known")
        hot_ready = sem("hot_ready")
        hot_used = sem("hot_used")
        tokens_found = sem("tokens_found")
        gather_ready = sem("gather_ready")
        rows_in = [sem(f"rows_in{s}") for s in range(RI)]
        rows_turned = sem("rows_turned")
        rows_hi = sem("rows_hi")
        rows_lo = sem("rows_lo")
        y_made = sem("y_made")
        y_biased = sem("y_biased")
        y_done = sem("y_done")
        y_out = [sem(f"y_out{s}") for s in range(4)]
        heads_zero = [sem(f"heads_zero{s}") for s in range(3)]
        pair_zero = sem("pair_zero")
        k_laid = [sem(f"k_laid{b}") for b in range(B)]
        q_laid = [sem(f"q_laid{b}") for b in range(B)]
        v_laid = sem("v_laid")
        lay_zero = sem("lay_zero")
        misc_filled = sem("misc_filled")
        misc_freed = [sem("misc_freed0"), sem("misc_freed1")]
        heads_in = [[sem(f"heads_in{s}_{g}") for g in range(G)] for s in range(3)]
        scores_ready = sem("scores_ready")
        max_done = sem("max_done")
        max_laid = sem("max_laid")
        logits_ready = sem("logits_ready")
        exp_done = sem("exp_done")
        pv_done = sem("pv_done")
        o_kept = sem("o_kept")
        o_laid = sem("o_laid")
        acc_in = [sem(f"acc_in{i}") for i in range(NT)]
        ya_in = [sem(f"ya_in{i}") for i in range(NT)]
        yb_in = [sem(f"yb_in{i}") for i in range(NT)]
        y_relu = sem("y_relu")
        half_bias = sem("half_bias")
        exp_table = sem("exp_table")
        res_out = [sem(f"res_out{s}") for s in range(4)]

        def misc_plan(b, u):
            plan = {0: ([], []),
                    1: ([("o", b - 1, 1)], [("max", 0, 1)] if b == 0 else []),
                    2: ([("k", b + 2, 0)], [("max", b, 1)] if b >= 1 else []),
                    3: ([("turn", b - 1, 0)], [("k", b + 2, 1)]),
                    4: ([("out", b - 1, 0)], [("out", b - 1, 1)]),
                    5: ([("o", b, 0)], [("out", b - 1, 2)]),
                    6: ([("out", b - 1, 3)], [("max", b + 1, 0)]),
                    7: ([("q", b + 2, 0)], [("q", b + 2, 1)])}[u]
            return [[j for j in half if 0 <= j[1] < B] for half in plan]

        FIRST = [("k", 0, 0), ("k", 0, 1), ("q", 0, 0), ("q", 0, 1)]

        def tile_jobs(n):
            return {MAX_AT: [("max", 0, 0)], K_AT: [("k", 1, 0), ("k", 1, 1)], Q_AT: [("q", 1, 0), ("q", 1, 1)]}.get(n, [])

        def tile_scores(n):
            return range(2 * (n - SCORES_AT), 2 * (n - SCORES_AT) + 2) if 0 <= n - SCORES_AT < H * QT // 2 else ()

        LAST = [("o", B - 1, 1), ("turn", B - 1, 0)] + [("out", B - 1, i) for i in range(QT)]
        misc = list(FIRST)
        for n in range(NS):
            misc += tile_jobs(n)
        for b in range(B):
            for u in range(2 * HG):
                for half in misc_plan(b, u):
                    misc += half
        misc += LAST
        misc_no = {job: n for n, job in enumerate(misc)}

        def wait_kept(eng, job):
            m = misc_no[job]
            eng.wait_ge(misc_freed[m % 2], m // 2 + 1)

        def wait_filled(eng, job):
            eng.wait_ge(misc_filled, misc_no[job] + 1)

        def score_bank(n):
            if n < H * QT:
                return (ps_s[:, 2, :], ps_o[:])[n % 2]
            return ps_s[:, n % RS, :]

        def unit_scores(b, u):
            n = 2 * HG * b + u - LAG
            return divmod(n + H, H) if 0 <= n < H * (B - 1) else None

        wp_ps = ps_m[:].rearrange("p a (c n) -> p (a c) n", c=2)[:, :, 0:3 * HD]

        def lay_out(eng, step, steps, b, which, tiles=range(QT)):
            s, first, hi_at, lo_at, laid = ((0, 0.0, (2, 10), 18, q_laid[b]) if which == "q" else
                                            (1, 1.0, (2, 18), 10, k_laid[b]))
            exact = proj[:, QT * b:QT * (b + 1), 0:2 * HD].rearrange("p i (h e s) -> p i h e s", e=HE, s=2)[:, :, :, :, s]
            heads = lay[(Q_LAY if which == "q" else K_LAY)[b]][:].rearrange("p i (h c) -> p i h c", c=32)
            for i in tiles:
                for at in hi_at:
                    eng.tensor_copy(heads[:, i, :, at:at + HE].bitcast(F32R), exact[:, i]).then_inc(step, 1)
                eng.memset(heads[:, i, :, 0:2], first).then_inc(step, 1)
                steps[0] += 3
            eng.wait_ge(step, steps[0])
            for i in tiles:
                eng.tensor_tensor(heads[:, i, :, lo_at:lo_at + HE], exact[:, i], heads[:, i, :, hi_at[0]:hi_at[0] + HE],
                                  ALU.subtract).then_inc(laid, 1)

        block = ctx.enter_context(nc.Block())

        @block.sync
        def _(sp):
            def load_x(i):
                if i >= RI:
                    sp.wait_ge(xn_made, i - RI + 1)
                sp.dma_start(row_in[:, i % RI, :], x_rows[i * P:(i + 1) * P, :]).then_inc(x_in[i % RI], 16)

            load_x(0)
            load_x(1)
            sp.dma_start(row_mid[:, 0, :], wqk).then_inc(weights_in, 16)
            sp.dma_start(row_mid[0:HD, 1, :], wv).then_inc(weights_in, 16)
            wo_src = wo.rearrange("(c p) k -> p c k", p=P)
            wo_dst = row_mid[:, 2, :].rearrange("p (c k) -> p c k", c=KC)
            sp.dma_start(wo_dst[:, :, 0:HD], wo_src).then_inc(weights_in, 16)
            sp.dma_start(wo_dst[:, :, HD:2 * HD], wo_src).then_inc(weights_in, 16)
            sp.dma_start(gate_w[:], wg.rearrange("(c p) e -> p c e", p=P)).then_inc(weights_in, 16)

            def load_w(c):
                if c >= RW:
                    sp.wait_ge(w_lo_made, c - RW + 1)
                e, half = divmod(c, 2)
                src = we[e].rearrange("(c p) h -> p c h", p=P)[:, 2 * half:2 * half + 2, :]
                sp.dma_start(stage[:, c % RW, :, :], src).then_inc(w_in[c % RW], 16)

            for i in range(2, RI):
                load_x(i)

            def row(ap):
                return ap.rearrange("(a d) -> a d", a=1).to_broadcast([P, ap.shape[0]])

            sp.dma_start(bias_p[:, 0:2 * HD], row(bqk)).then_inc(biases_in, 16)
            sp.dma_start(bias_p[:, 2 * HD:3 * HD], row(bv)).then_inc(biases_in, 16)
            sp.dma_start(bias_p[:, 3 * HD:PW], row(bg)).then_inc(biases_in, 16)
            sp.dma_start(bias_o[:], row(bo)).then_inc(biases_in, 16)
            for c in range(RW):
                load_w(c)
            for i in range(NT):
                sp.wait_ge(xn_made, i + 1)
                sp.dma_start(xn_dram[i * P:(i + 1) * P, :], row_mid[:, i % 4, :]).then_inc(xn_out[i % 4], 16)
                if i + RI < NT:
                    load_x(i + RI)
                if RW <= i + RW - 2 < NT:
                    load_w(i + RW - 2)
            sp.wait_ge(projected, NT)
            sp.wait_ge(proj_kept, NT)
            sp.wait_ge(w_lo_made, 2 * NE)
            sp.wait_ge(w_hi_made, 2 * NE)
            sp.dma_start(bias_e[:], be.rearrange("(a e) h -> a e h", a=1).to_broadcast([P, NE, F])).then_inc(bias_e_in, 16)

            def load_heads(b, g):
                wait_kept(sp, ("k", b, g))
                if b < 3:
                    sp.wait_ge(heads_zero[b], 2 * (g + 1) - (b == 1))
                    if b == 1:
                        sp.wait_ge(pair_zero, 1)
                else:
                    sp.wait_ge(logits_ready, (b - 2) * 2 * HG * HG)
                for j in range(HG):
                    rows = slice(32 * j, 32 * j + 32)
                    sp.dma_start(k_head[b % 3][rows, g * HG + j, :].bitcast(F32), k_t[b % 2][rows, g, :].bitcast(F32)).then_inc(heads_in[b % 3][g], 16)

            for n in range(NS):
                if n == NS - 1:
                    load_heads(1, 0)
                sp.wait_ge(y_done, n + 1)
                sp.dma_start(y_dram[n * P:(n + 1) * P, :], row_mid[:, n % 4, :]).then_inc(y_out[n % 4], 16)
                if n in COPY_AT:
                    load_heads(0, COPY_AT.index(n))

            def load_acc(i):
                sp.dma_start(acc[:, i, :], x_rows[i * P:(i + 1) * P, :]).then_inc(acc_in[i], 16)

            def store(i):
                wait_kept(sp, ("out", i // QT, i % QT))
                sp.dma_start(out_rows[i * P:(i + 1) * P, :], res[:, i % 4, :]).then_inc(res_out[i % 4], 16)

            load_heads(1, 1)
            sp.wait_ge(y_made, NS)
            for i in range(QT):
                load_acc(i)
            for g in range(G):
                load_heads(2, g)
            for i in range(QT, NT):
                load_acc(i)
            for g in range(G):
                load_heads(3, g)
            for i in range(NT):
                store(i)
            for s in range(4):
                sp.wait_ge(res_out[s], 16 * NT // 4)

        @block.gpsimd
        def _(pool):
            steps = [0]

            def link(ins):
                steps[0] += 1
                ins.then_inc(pool_step, 1)
                pool.wait_ge(pool_step, steps[0])

            link(pool.memset(ident[:], 0.0))
            pool.affine_select(out=ident[:], in_=ident[:], compare_op=ALU.not_equal, fill=1.0, base=0,
                               pattern=[[-1, P]], channel_multiplier=1).then_inc(consts_ready, 1)
            pool.memset(eps_t[:], EPS).then_inc(consts_ready, 1)
            link(pool.memset(ones[:], 1.0))
            pool.affine_select(out=before[:], in_=ones[:], compare_op=ALU.is_gt, fill=0.0, base=0,
                               pattern=[[1, P]], channel_multiplier=-1).then_inc(consts_ready, 1)
            link(pool.iota(ramp_i[:], pattern=[[1, P]], base=0, channel_multiplier=0))
            pool.tensor_copy(ramp[:], ramp_i[:]).then_inc(consts_ready, 1)
            link(pool.iota(part_i[:], pattern=[[0, 1]], base=0, channel_multiplier=1))
            pool.tensor_copy(part[:], part_i[:]).then_inc(consts_ready, 1)
            link(pool.memset(lower[:], 1.0))
            pool.affine_select(out=lower[:], in_=lower[:], compare_op=ALU.is_gt, fill=0.0, base=0,
                               pattern=[[1, NE], [-1, NE]], channel_multiplier=0).then_inc(consts_ready, 1)

            for c in range(2 * NE):
                e, half = divmod(c, 2)
                pool.wait_ge(w_in[c % RW], 16 * (c // RW + 1))
                pool.wait_ge(w_hi_made, c + 1)
                cs = slice(2 * half, 2 * half + 2)
                pool.tensor_tensor(w_split[:, e, 1, cs, :], stage[:, c % RW, :, :], w_split[:, e, 0, cs, :].bitcast(F32),
                                   ALU.subtract).then_inc(w_lo_made, 1)

            pool.wait_ge(w_hi_made, 2 * NE)
            pool.wait_ge(w_lo_made, 2 * NE)
            pool.wait_ge(projected, NT)
            pool.wait_ge(proj_kept, NT)
            link(pool.memset(lay_0[:], 0.0))
            lay_out(pool, pool_step, steps, 0, "k")
            for g in range(G):
                wait_filled(pool, ("k", 0, g))
            lay_out(pool, pool_step, steps, 0, "q")

            for s in range(4):
                pool.wait_ge(xn_out[s], 16 * NT // 4)
            pool.wait_ge(xn_made, NT)
            pool.wait_ge(gather_ready, 1)

            def gather(n):
                if n >= RI:
                    pool.wait_ge(rows_turned, n - RI + 1)
                pool.indirect_dma_start(row_in[:, n % RI, :], None, xn_dram,
                                        bass.IndirectOffsetOnAxis(ap=gather_i[:, n:n + 1], axis=0)).then_inc(rows_in[n % RI], 16)

            for n in range(RI):
                gather(n)
            pool.wait_ge(biases_in, 64)
            pool.tensor_scalar(bias_o[:], bias_o[:], 0.5, None, ALU.mult).then_inc(half_bias, 1)
            pool.wait_ge(half_bias, 1)
            for n in range(NS):
                if n == NS - 1:
                    pool.wait_ge(y_biased, NS)
                    pool.memset(k_head1[:, 2:4, :].bitcast(F32), 0.0).then_inc(heads_zero[1], 1)
                pool.wait_ge(y_relu, n + 1)
                pool.tensor_tensor(row_mid[:, n % 4, :], row_mid[:, n % 4, :], bias_o[:], ALU.add).then_inc(y_done, 1)
                if n + RI < NS:
                    gather(n + RI)
                if n == FREE_1 - 1:
                    pool.wait_ge(y_made, FREE_1)
                    pool.memset(lay_2[:], 0.0).then_inc(lay_zero, 1)
                    pool.memset(lay_1[:], 0.0).then_inc(lay_zero, 1)

            pool.wait_ge(y_made, NS)
            pool.wait_ge(y_biased, NS)
            for hs in (slice(4, 6), slice(6, 8)):
                pool.memset(k_head1[:, hs, :].bitcast(F32), 0.0).then_inc(heads_zero[1], 1)
            for h in range(0, H, 2):
                pool.memset(k_head2[:, h:h + 2, :].bitcast(F32), 0.0).then_inc(heads_zero[2], 1)
            wait_filled(pool, ("max", 0, 1))
            lay_out(pool, pool_step, steps, 3, "k")
            for s in range(4):
                pool.wait_ge(y_out[s], 16 * ((NS - s + 3) // 4))

            def add_rows(i, r, before_it, landed):
                pool.wait_ge(before_it[i], 16)
                pool.indirect_dma_start(acc[:, i, :], None, y_dram,
                                        bass.IndirectOffsetOnAxis(ap=slots_i[:, r, i:i + 1], axis=0),
                                        compute_op=ALU.add).then_inc(landed[i], 16)

            for i in range(NT + 2):
                if i < NT:
                    add_rows(i, 0, acc_in, ya_in)
                if i >= 2:
                    add_rows(i - 2, 1, ya_in, yb_in)
                if i == NT // 2:
                    wait_filled(pool, ("k", 2, 1))
                    lay_out(pool, pool_step, steps, 3, "q")

        @block.scalar
        def _(act):
            act.wait_ge(consts_ready, 2)

            def split_w(c):
                e, half = divmod(c, 2)
                act.wait_ge(w_in[c % RW], 16 * (c // RW + 1))
                act.activation(w_split[:, e, 0, 2 * half:2 * half + 2, :], stage[:, c % RW, :, :],
                               ACT.Copy).then_inc(w_hi_made, 1)

            def hi(i):
                act.wait_ge(turned, i + 1)
                if i >= 2:
                    act.wait_ge(projected, i - 1)
                act.activation(t_hi[:, i % 2, :], ps_t[:, i % 2, :], ACT.Copy).then_inc(hi_made, 1)

            def root(g):
                act.wait_ge(var_ready, g + 1)
                act.activation(small[:, 1, 2 * g:2 * g + 2], small[:, 0, 2 * g:2 * g + 2], ACT.Sqrt).then_inc(root_ready, 1)

            root(0)
            act.wait_ge(weights_turned, 1)
            act.activation(wp_hi[:, :, 0:3 * HD], wp_ps, ACT.Copy).then_inc(weights_split, 1)
            act.wait_ge(weights_in, 80)
            act.activation(wp_hi[:, :, 3 * HD:PW], gate_w[:], ACT.Copy).then_inc(weights_split, 1)
            for i in range(NT):
                act.wait_ge(norm_ready, i // 2 + 1)
                act.wait_ge(x_in[i % RI], 16 * (i // RI + 1))
                if i == 0:
                    act.wait_ge(weights_turned, 2)
                if i == 1:
                    act.activation(wo_hi[:], ps_s[:, 2, :], ACT.Copy).then_inc(weights_split, 1)
                if i >= 4:
                    act.wait_ge(turned, i - 3)
                    act.wait_ge(xn_out[i % 4], 16 * (i // 4))
                act.activation(row_mid[:, i % 4, :], row_in[:, i % RI, :], ACT.Identity,
                               bias=small[:, 6, i:i + 1], scale=small[:, 5, i:i + 1]).then_inc(xn_made, 1)
                if i >= 1:
                    hi(i - 1)
                if i % 2 == 1 and i + 1 < NT:
                    root(i // 2 + 1)
                split_w(i)
            hi(NT - 1)

            def rows_high(n):
                act.wait_ge(rows_turned, n + 1)
                if n >= 2:
                    act.wait_ge(y_made, n - 1)
                act.activation(t_hi[:, n % 2, :], ps_t[:, n % 2, :], ACT.Copy).then_inc(rows_hi, 1)

            def relu(n):
                act.wait_ge(y_biased, n + 1)
                act.activation(row_mid[:, n % 4, :], row_mid[:, n % 4, :], ACT.Relu, scale=0.5).then_inc(y_relu, 1)

            def keep(kind, b, g):
                m = misc_no[(kind, b, g)]
                act.wait_ge(misc_filled, m + 1)
                if kind == "k":
                    if b >= 2:
                        for part in range(G):
                            act.wait_ge(heads_in[(b - 2) % 3][part], 16 * HG * ((b - 2) // 3 + 1))
                    dst = k_t[b % 2][:, g, :]
                elif kind == "q":
                    if b >= 3:
                        act.wait_ge(logits_ready, HG * 2 * HG * (b - 2))
                    dst = q_t[b % 3][:, g, :]
                elif kind == "max":
                    dst = q_t[b % 3][:, g, :]
                else:
                    if b >= 1:
                        wait_filled(act, ("out", b - 1, QT - 1))
                    dst = o_t[:]
                act.activation(dst, ps_m[:, m % 2, :], ACT.Copy).then_inc(misc_freed[m % 2], 1)

            KEPT = ("k", "q", "max", "turn")
            act.activation(small[:, 7, 0:1], eps_t[:], ACT.Exp).then_inc(exp_table, 1)
            for job in FIRST:
                keep(*job)
            for n in range(NS + 1):
                if n < NS:
                    rows_high(n)
                if n >= 1:
                    relu(n - 1)
                    for job in tile_jobs(n - 1):
                        keep(*job)

            def keep_o(b, g):
                act.wait_ge(pv_done, 2 * HG * b + HG * (g + 1))
                if 2 * b + g >= 2:
                    wait_filled(act, ("o", b - 1, g))
                act.activation(o_sum[:, g, :], ps_o[:], ACT.Copy).then_inc(o_kept, 1)

            for b in range(B):
                for u in range(2 * HG):
                    n = 2 * HG * b + u
                    mid, end = misc_plan(b, u)
                    for j in range(HG):
                        act.wait_ge(logits_ready, HG * n + j + 1)
                        if j == 0 and n >= 2:
                            act.wait_ge(pv_done, n - 1)
                        act.activation(probs[:, n % 2, j, :], ps_t[:, j % 2, :], ACT.Exp).then_inc(exp_done, 1)
                        if j == 1:
                            if u == 0 and b >= 1:
                                keep_o(b - 1, 1)
                            if u == HG:
                                keep_o(b, 0)
                            for job in mid:
                                if job[0] in KEPT:
                                    keep(*job)
                    for job in end:
                        if job[0] in KEPT:
                            keep(*job)
            keep_o(B - 1, 1)
            keep("turn", B - 1, 0)

        @block.vector
        def _(dve):
            steps = [0]

            def link(ins):
                steps[0] += 1
                ins.then_inc(dve_step, 1)
                dve.wait_ge(dve_step, steps[0])

            dve.memset(ps_o[:], 0.0).then_inc(dve_step, 1)
            steps[0] += 1
            def moments(g):
                for i in (2 * g, 2 * g + 1):
                    dve.wait_ge(x_in[i % RI], 16 * (i // RI + 1))
                    dve.bn_stats(stats[:, g % 2, i % 2, :], row_in[:, i % RI, :]).then_inc(dve_step, 1)
                    steps[0] += 1
                for i in (2 * g, 2 * g + 1):
                    dve.wait_ge(dve_step, steps[0] - 1 + i % 2 if i % 2 else steps[0] - 1)
                    dve.bn_aggr(mv[:, i, :], stats[:, g % 2, i % 2, :]).then_inc(dve_step, 1)
                    steps[0] += 1
                dve.wait_ge(dve_step, steps[0])
                ts = slice(2 * g, 2 * g + 2)
                dve.tensor_scalar(small[:, 0, ts], mv[:, ts, 1], EPS, None, ALU.add).then_inc(var_ready, 1)

            def scales(g):
                ts = slice(2 * g, 2 * g + 2)
                d, r, a, c = (small[:, k, ts] for k in (0, 2, 3, 4))
                dve.wait_ge(var_ready, g + 1)
                dve.wait_ge(root_ready, g + 1)
                link(dve.reciprocal(r, small[:, 1, ts]))
                link(dve.tensor_tensor(a, r, r, ALU.mult))
                link(dve.tensor_tensor(c, a, d, ALU.mult))
                link(dve.tensor_scalar(a, c, -0.5, 1.5, ALU.mult, ALU.add))
                link(dve.tensor_tensor(small[:, 5, ts], r, a, ALU.mult))
                dve.scalar_tensor_tensor(out=small[:, 6, ts], in0=mv[:, ts, 0], scalar=-1.0,
                                         in1=small[:, 5, ts], op0=ALU.mult, op1=ALU.mult).then_inc(norm_ready, 1)

            def low(i):
                dve.wait_ge(hi_made, i + 1)
                if i >= 2:
                    dve.wait_ge(projected, i - 1)
                dve.tensor_tensor(t_lo[:, i % 2, :], ps_t[:, i % 2, :], t_hi[:, i % 2, :].bitcast(F32),
                                  ALU.subtract).then_inc(lo_made, 1)

            def keep_proj(i):
                dve.wait_ge(projected, i + 1)
                if i == 0:
                    dve.wait_ge(biases_in, 64)
                dve.tensor_tensor(proj[:, i, :], ps_s[:, i % 2, 0:PW], bias_p[:], ALU.add).then_inc(proj_kept, 1)

            def top(i):
                dve.wait_ge(proj_kept, i + 1)
                logits = proj[:, i, 3 * HD:PW]
                link(dve.max(top_v[:, i, :], logits))
                dve.max_index(top_i[:, i, :], top_v[:, i, :], logits).then_inc(dve_step, 1)
                steps[0] += 1

            moments(0)
            scales(0)
            moments(1)
            dve.wait_ge(weights_turned, 1)
            dve.wait_ge(weights_split, 2)
            dve.tensor_tensor(wp_lo[:, :, 0:3 * HD], wp_ps, wp_hi[:, :, 0:3 * HD].bitcast(F32), ALU.subtract).then_inc(weights_split, 1)
            dve.tensor_tensor(wp_lo[:, :, 3 * HD:PW], gate_w[:], wp_hi[:, :, 3 * HD:PW].bitcast(F32),
                              ALU.subtract).then_inc(weights_split, 1)
            for i in range(NT):
                low(i)
                if i % 2 == 0 and i + 2 < NT:
                    scales(i // 2 + 1)
                if i % 2 == 1 and i + 3 < NT:
                    moments(i // 2 + 2)
                if i == 1:
                    dve.wait_ge(weights_split, 5)
                    dve.tensor_tensor(wo_lo[:], ps_s[:, 2, :], wo_hi[:].bitcast(F32), ALU.subtract).then_inc(weights_split, 1)
                if i >= 1:
                    keep_proj(i - 1)
                if i >= 1:
                    top(i - 1)
            keep_proj(NT - 1)
            top(NT - 1)

            dve.wait_ge(dve_step, steps[0])
            link(dve.tensor_copy(top_f[:], top_i[:]))
            dve.wait_ge(consts_ready, 6)
            ramp8 = ramp[:, 0:NE].unsqueeze(1).to_broadcast([P, NT, NE])
            for r in range(2):
                ins = dve.tensor_tensor(pick[:, r], ramp8, top_f[:, :, r:r + 1].to_broadcast([P, NT, NE]), ALU.is_equal)
                ins.then_inc(dve_step, 1)
                steps[0] += 1
            dve.memset(mask[:, NT, :], 0.0).then_inc(mask_ready, 1)
            dve.wait_ge(dve_step, steps[0])
            dve.tensor_tensor(mask[:, 0:NT, :], pick[:, 0], pick[:, 1], ALU.add).then_inc(mask_ready, 1)

            link(dve.tensor_scalar(token_f[:], ramp[:, 0:NT], float(P), None, ALU.mult))
            link(dve.tensor_scalar(token_f[:], token_f[:], part[:, 0:1], None, ALU.add))

            dve.wait_ge(counted, 1)
            ps_c = ps_s[:, 0, 0:(NT + 1) * NE].rearrange("p (i e) -> p i e", e=NE)
            thresholds = ramp[:, 0:NT].unsqueeze(1).to_broadcast([P, NE, NT])
            link(dve.scalar_tensor_tensor(out=tiles_gt[:], in0=ps_c[:, NT, :].unsqueeze(2).to_broadcast([P, NE, NT]), scalar=1.0 / P,
                                          in1=thresholds, op0=ALU.mult, op1=ALU.is_gt))
            link(dve.tensor_reduce(ecol[:, 1, :], tiles_gt[:], AX.X, ALU.add))
            link(dve.tensor_tensor(tri[:], lower[:], ecol[:, 1:2, :].to_broadcast([P, NE, NE]), ALU.mult))
            link(dve.tensor_reduce(ecol[:, 2, :], tri[:], AX.X, ALU.add))
            link(dve.tensor_scalar(ecol[:, 0, :], ecol[:, 2, :], float(P), None, ALU.mult))
            link(dve.tensor_tensor(place[:, 0:NT, :], ps_c[:, 0:NT, :], ecol[:, 0:1, :].to_broadcast([P, NT, NE]), ALU.add))
            for r in range(2):
                dve.tensor_tensor(slot_p[:, r], place[:, 0:NT, :], pick[:, r], ALU.mult).then_inc(dve_step, 1)
            steps[0] += 2
            dve.wait_ge(dve_step, steps[0])
            link(dve.tensor_reduce(slot_f[:], slot_p[:], AX.X, ALU.add))
            link(dve.tensor_copy(slots_i[:], slot_f[:]))
            dve.tensor_scalar(slot_r[:, 0], slots_i[:], P - 1, None, ALU.bitwise_and).then_inc(dve_step, 1)
            dve.tensor_scalar(slot_r[:, 1], slots_i[:], P.bit_length() - 1, None, ALU.arith_shift_right).then_inc(dve_step, 1)
            steps[0] += 2
            dve.wait_ge(dve_step, steps[0])
            link(dve.tensor_copy(slot_q[:], slot_r[:].rearrange("p a r i -> p a (r i)")))
            link(dve.tensor_tensor(hot_tile[:], ramp[:, 0:NSE].unsqueeze(1).to_broadcast([P, NC, NSE]),
                                   slot_q[:, 1, :].unsqueeze(2).to_broadcast([P, NC, NSE]), ALU.is_equal))
            for c in range(0, NC, 4):
                at, i = (c // 4) % 3, c % NT
                if c >= 12:
                    dve.wait_ge(hot_used, c // 4 - 2)
                dve.tensor_tensor(hot_val[:, at], hot_tile[:, c:c + 4, :], token_f[:, i:i + 4].unsqueeze(2).to_broadcast([P, 4, NSE]),
                                  ALU.mult).then_inc(hot_ready, 1)
                dve.tensor_tensor(hot_row[:, at], ramp[:].unsqueeze(1).to_broadcast([P, 4, P]),
                                  slot_q[:, 0, c:c + 4].unsqueeze(2).to_broadcast([P, 4, P]), ALU.is_equal).then_inc(hot_ready, 1)
            link(dve.tensor_tensor(ecol[:, 3, :], ecol[:, 1, :], ecol[:, 2, :], ALU.add))
            link(dve.tensor_tensor(te_cmp[:], ecol[:, 3:4, :].to_broadcast([P, NS, NE]),
                                   ramp[:, 0:NS].unsqueeze(2).to_broadcast([P, NS, NE]), ALU.is_le))
            link(dve.tensor_reduce(te_f[:], te_cmp[:], AX.X, ALU.add))
            dve.tensor_scalar(expert_i[:], te_f[:], float(NE - 1), None, ALU.min).then_inc(experts_known, 1)
            dve.wait_ge(tokens_found, 1)
            dve.tensor_copy(gather_i[:], ps_s[:, 1, 0:NS]).then_inc(gather_ready, 1)

            def rows_low(n):
                dve.wait_ge(rows_hi, n + 1)
                dve.tensor_tensor(t_lo[:, n % 2, :], ps_t[:, n % 2, :], t_hi[:, n % 2, :].bitcast(F32),
                                  ALU.subtract).then_inc(rows_lo, 1)

            dve.wait_ge(experts_known, 1)
            dve.wait_ge(bias_e_in, 16)
            def maximum(b, h, i):
                n = QT * (H * b + h) + i
                dve.wait_ge(scores_ready, n + 1)
                if b >= 2 and h == 0 and i == 0:
                    dve.wait_ge(max_laid, 2 * (b - 1))
                dve.tensor_reduce(row_max[:, b % 2, h, i:i + 1], score_bank(n), AX.X, ALU.max).then_inc(max_done, 1)

            def lay_max(b, g):
                dve.wait_ge(max_done, QT * (H * b + HG * (g + 1)))
                dve.wait_ge(q_laid[b], QT)
                mx = row_max[:, b % 2, HG * g:HG * (g + 1), :].rearrange("p h i -> p i h")
                heads = lay[Q_LAY[b]][:].rearrange("p i (h c) -> p i h c", c=32)[:, :, HG * g:HG * (g + 1), :]
                link(dve.tensor_scalar(heads[:, :, :, 0].bitcast(F32R), mx, -1.0, None, ALU.mult))
                dve.scalar_tensor_tensor(out=heads[:, :, :, 1], in0=mx, scalar=-1.0, in1=heads[:, :, :, 0],
                                         op0=ALU.mult, op1=ALU.subtract).then_inc(max_laid, 1)

            for n in range(NS + 1):
                if n < NS:
                    rows_low(n)
                if n >= 1:
                    e = dve.value_load(expert_i[0:1, n - 1:n], min_val=0, max_val=NE - 1)
                    dve.wait_ge(y_made, n)
                    if n > 4:
                        dve.wait_ge(y_out[(n - 1) % 4], 16 * ((n - 1) // 4))
                    dve.tensor_tensor(row_mid[:, (n - 1) % 4, :], ps_s[:, (n - 1) % 2, :], bias_e[:, bass.ds(e, 1), :].rearrange("p a h -> p (a h)"),
                                      ALU.add).then_inc(y_biased, 1)
                    if 0 <= n - ZERO_AT < 4:
                        hs = slice(2 * (n - ZERO_AT), 2 * (n - ZERO_AT) + 2)
                        dve.memset(k_head0[:, hs, :].bitcast(F32), 0.0).then_inc(heads_zero[0], 1)
                    for s in tile_scores(n - 1):
                        maximum(0, s // QT, s % QT)
                    if n == MAX_AT:
                        lay_max(0, 0)
                    if 0 <= n - LAY_AT < QT:
                        dve.wait_ge(lay_zero, 2)
                        for which in ("k", "q"):
                            lay_out(dve, dve_step, steps, 1, which, (n - LAY_AT,))

            dve.wait_ge(y_biased, NS)
            dve.memset(k_head1[:, 0:2, :].bitcast(F32), 0.0).then_inc(pair_zero, 1)
            lay_max(0, 1)
            dve.memset(v_ones[:, :, :, HE:VC], float(HD) ** 0.5).then_inc(v_laid, 1)
            for b in range(B):
                ts = slice(QT * b, QT * (b + 1))
                dve.tensor_copy(v_ones[:, ts, :, 0:HE],
                                proj[:, ts, 2 * HD:3 * HD].rearrange("p i (h e) -> p i h e", e=HE)).then_inc(v_laid, 1)
            link(dve.memset(lay_3[:], 0.0))
            lay_out(dve, dve_step, steps, 2, "k")
            wait_filled(dve, ("k", 1, 1))
            lay_out(dve, dve_step, steps, 2, "q")

            def lay_o(b, g):
                m = misc_no[("o", b, g)]
                dve.wait_ge(misc_filled, m + 1)
                sums = ps_m[:, m % 2, :].rearrange("p (i j c) -> p i j c", j=HG, c=32)
                if b >= 1 and g == 0:
                    wait_filled(dve, ("turn", b - 1, 0))
                link(dve.reciprocal(o_inv[:], sums[:, :, :, HE]))
                cs = slice(g * HG * HE, (g + 1) * HG * HE)
                exact = o_exact[:, :, cs].rearrange("p i (j e) -> p i j e", e=HE)
                for i in range(QT - 1):
                    dve.tensor_tensor(exact[:, i], sums[:, i, :, 0:HE], o_inv[:, i, :].unsqueeze(2).to_broadcast([P, HG, HE]), ALU.mult).then_inc(dve_step, 1)
                    steps[0] += 1
                i = QT - 1
                dve.tensor_tensor(exact[:, i], sums[:, i, :, 0:HE], o_inv[:, i, :].unsqueeze(2).to_broadcast([P, HG, HE]), ALU.mult).then_inc(misc_freed[m % 2], 1)
                dve.wait_ge(dve_step, steps[0])
                dve.wait_ge(misc_freed[m % 2], m // 2 + 1)
                link(dve.tensor_copy(o_tok[:, :, cs].bitcast(F32R), o_exact[:, :, cs]))
                dve.tensor_tensor(o_tok[:, :, HD + g * HG * HE:HD + (g + 1) * HG * HE], o_exact[:, :, cs],
                                  o_tok[:, :, cs], ALU.subtract).then_inc(o_laid, 1)

            def result(b, i):
                n = QT * b + i
                m = misc_no[("out", b, i)]
                dve.wait_ge(yb_in[n], 16)
                if n >= 4:
                    dve.wait_ge(res_out[n % 4], 16 * (n // 4))
                dve.wait_ge(misc_filled, m + 1)
                dve.tensor_tensor(res[:, n % 4, :], ps_m[:, m % 2, :], acc[:, n, :], ALU.add).then_inc(misc_freed[m % 2], 1)

            def serve(jobs):
                for kind, b, g in jobs:
                    if kind == "o":
                        lay_o(b, g)
                    elif kind == "out":
                        result(b, g)

            for b in range(B):
                for u in range(2 * HG):
                    mid, end = misc_plan(b, u)
                    head = unit_scores(b, u)
                    for half, jobs in enumerate((mid, end)):
                        if head:
                            maximum(head[0], head[1], 2 * half)
                            maximum(head[0], head[1], 2 * half + 1)
                        serve(jobs)
                    if head and head[1] % HG == HG - 1:
                        lay_max(head[0], head[1] // HG)
            serve(LAST)

        @block.tensor
        def _(pe):
            pe.wait_ge(consts_ready, 1)
            pe.wait_ge(weights_in, 80)
            for c in range(KC):
                pe.transpose(ps_m[:, c // 2, (c % 2) * 256:(c % 2) * 256 + P], row_mid[:, 0, c * P:(c + 1) * P], ident[:])
                mm = pe.transpose(ps_m[:, c // 2, (c % 2) * 256 + P:(c % 2) * 256 + P + HD], row_mid[0:HD, 1, c * P:(c + 1) * P],
                                  ident[0:HD, 0:HD])
            mm.then_inc(weights_turned, 1)
            for c in range(KC):
                mm = pe.transpose(ps_s[:, 2, c * P:(c + 1) * P], row_mid[:, 2, c * P:(c + 1) * P], ident[:])
            mm.then_inc(weights_turned, 1)

            def turn(i):
                pe.wait_ge(xn_made, i + 1)
                if i >= 2:
                    pe.wait_ge(lo_made, i - 1)
                for c in range(KC):
                    mm = pe.transpose(ps_t[:, i % 2, c * P:(c + 1) * P], row_mid[:, i % 4, c * P:(c + 1) * P], ident[:])
                mm.then_inc(turned, 1)

            def project(i):
                pe.wait_ge(hi_made, i + 1)
                pe.wait_ge(lo_made, i + 1)
                if i == 0:
                    pe.wait_ge(weights_split, 4)
                if i >= 2:
                    pe.wait_ge(proj_kept, i - 1)
                n = 0
                for c in range(KC):
                    ks = slice(c * P, (c + 1) * P)
                    for a, w in ((t_hi, wp_hi), (t_hi, wp_lo), (t_lo, wp_hi)):
                        mm = pe.matmul(ps_s[:, i % 2, 0:PW], a[:, i % 2, ks], w[:, c, :], start=(n == 0), stop=(n == 3 * KC - 1))
                        n += 1
                mm.then_inc(projected, 1)

            for i in range(NT):
                turn(i)
                if i >= 1:
                    project(i - 1)
            project(NT - 1)

            def fill(kind, b, g):
                m = misc_no[(kind, b, g)]
                if m >= 2:
                    pe.wait_ge(misc_freed[m % 2], m // 2)
                bank = ps_m[:, m % 2, :]
                if kind in ("k", "q", "max"):
                    if kind == "k":
                        pe.wait_ge(k_laid[b], QT)
                    elif kind == "q":
                        pe.wait_ge(q_laid[b], QT)
                    else:
                        pe.wait_ge(max_laid, 2 * b + g + 1)
                    src = lay[(K_LAY if kind == "k" else Q_LAY)[b]]
                    for i in range(QT):
                        mm = pe.transpose(bank[:, i * P:(i + 1) * P], src[:, i, g * P:(g + 1) * P], ident[:])
                elif kind == "o":
                    pe.wait_ge(o_kept, 2 * b + g + 1)
                    for i in range(QT):
                        mm = pe.transpose(bank[:, i * P:(i + 1) * P], o_sum[:, g, i * P:(i + 1) * P], ident[:])
                elif kind == "turn":
                    pe.wait_ge(o_laid, 2 * b + 2)
                    for i in range(QT):
                        mm = pe.transpose(bank[:, i * P:(i + 1) * P], o_tok[:, i, :], ident[:])
                else:
                    wait_kept(pe, ("turn", b, 0))
                    ts = slice(g * P, (g + 1) * P)
                    pe.matmul(bank, o_t[:, ts], wo_hi[:], start=True, stop=False)
                    mm = pe.matmul(bank, o_t[:, ts], wo_lo[:], start=False, stop=True)
                mm.then_inc(misc_filled, 1)

            def scores(b, h, i):
                n = QT * (H * b + h) + i
                if i == 0 and h % HG == 0:
                    pe.wait_ge(heads_in[b % 3][h // HG], 16 * HG * (b // 3 + 1))
                    wait_kept(pe, ("q", b, h // HG))
                if H * QT <= n < H * QT + RS:
                    pe.wait_ge(max_done, H * QT)
                elif n >= RS:
                    pe.wait_ge(max_done, n + 1 - (RS if n >= H * QT else 2))
                elif n == 2:
                    pe.wait_ge(max_done, 1)
                pe.matmul(score_bank(n), q_t[b % 3][:, h // HG, i * P:(i + 1) * P], k_head[b % 3][:, h, :],
                          start=True, stop=True).then_inc(scores_ready, 1)

            def logits(b, u, j):
                g, kt = divmod(u, QT)
                n = HG * (2 * HG * b + u) + j
                if n >= 2:
                    pe.wait_ge(exp_done, n - 1)
                if kt == 0 and j == 0:
                    wait_kept(pe, ("max", b, g))
                pe.matmul(ps_t[:, n % 2, :], k_head[b % 3][:, g * HG + j, kt * P:(kt + 1) * P], q_t[b % 3][:, g, :],
                          start=True, stop=True).then_inc(logits_ready, 1)

            def values(b, u):
                g, kt = divmod(u, QT)
                n = 2 * HG * b + u
                pe.wait_ge(exp_done, HG * (n + 1))
                pe.wait_ge(v_laid, b + 2)
                if n == 0:
                    pe.wait_ge(max_done, H * QT)
                if kt == 0 and n > 0:
                    pe.wait_ge(o_kept, 2 * b + g)
                for j in range(HG):
                    mm = pe.matmul(ps_o[32 * j:32 * j + VC, :], v_ones[:, QT * b + kt, g * HG + j, :], probs[:, n % 2, j, :],
                                   start=(kt == 0), stop=(kt == QT - 1))
                mm.then_inc(pv_done, 1)

            pe.wait_ge(mask_ready, 2)
            counts = ps_s[:, 0, 0:(NT + 1) * NE].rearrange("p (i e) -> p i e", e=NE)
            pe.matmul(counts[:, :, :], before[:], mask[:, :, :], start=True, stop=False)
            for i in range(NT):
                later = NT - i
                mm = pe.matmul(counts[:, i + 1:NT + 1, :], ones[:], mask[:, i:i + 1, :].to_broadcast([P, later, NE]),
                               start=False, stop=(i == NT - 1))
            mm.then_inc(counted, 1)
            for job in FIRST[:2]:
                fill(*job)
            for c in range(NC):
                if c % 4 == 0:
                    pe.wait_ge(hot_ready, 2 * (c // 4 + 1))
                at = (c // 4) % 3, c % 4
                mm = pe.matmul(ps_s[:, 1, 0:NSE], hot_row[:, at[0], at[1], :], hot_val[:, at[0], at[1], :], start=(c == 0), stop=(c == NC - 1))
                if c % 4 == 3 and c < NC - 1:
                    mm.then_inc(hot_used, 1)
            mm.then_inc(tokens_found, 1)
            for job in FIRST[2:]:
                fill(*job)

            def turn_rows(n):
                pe.wait_ge(rows_in[n % RI], 16 * (n // RI + 1))
                if n >= 2:
                    pe.wait_ge(rows_lo, n - 1)
                for c in range(KC):
                    mm = pe.transpose(ps_t[:, n % 2, c * P:(c + 1) * P], row_in[:, n % RI, c * P:(c + 1) * P], ident[:])
                mm.then_inc(rows_turned, 1)

            pe.wait_ge(experts_known, 1)
            pe.wait_ge(w_hi_made, 2 * NE)
            pe.wait_ge(w_lo_made, 2 * NE)
            turn_rows(0)
            for n in range(NS):
                e = pe.value_load(expert_i[0:1, n:n + 1], min_val=0, max_val=NE - 1)
                if n + 1 < NS:
                    turn_rows(n + 1)
                pe.wait_ge(rows_hi, n + 1)
                pe.wait_ge(rows_lo, n + 1)
                if n >= 2:
                    pe.wait_ge(y_biased, n - 1)
                k = 0
                for c in range(KC):
                    ks = slice(c * P, (c + 1) * P)
                    for a, w in ((t_hi, 0), (t_hi, 1), (t_lo, 0)):
                        rhs = w_split[:, bass.ds(e, 1), w, c, :].rearrange("p a h -> p (a h)")
                        mm = pe.matmul(ps_s[:, n % 2, :], a[:, n % 2, ks], rhs, start=(k == 0), stop=(k == 3 * KC - 1))
                        k += 1
                mm.then_inc(y_made, 1)
                for s in tile_scores(n):
                    scores(0, s // QT, s % QT)
                for job in tile_jobs(n):
                    fill(*job)

            pe.wait_ge(rows_lo, NS)
            for b in range(B):
                for u in range(2 * HG):
                    mid, end = misc_plan(b, u)
                    head = unit_scores(b, u)
                    for half, jobs in enumerate((mid, end)):
                        for j in (2 * half, 2 * half + 1):
                            logits(b, u, j)
                            if head:
                                scores(head[0], head[1], j)
                        for job in jobs:
                            fill(*job)
                        if half == 0 and u >= 1:
                            values(b, u - 1)
                        elif half == 0 and b >= 1:
                            values(b - 1, 2 * HG - 1)
            values(B - 1, 2 * HG - 1)
            for job in LAST:
                fill(*job)

_INS = ['L0_attn_x', 'L0_attn_Wqk_w', 'L0_attn_Wqk_b', 'L0_attn_Wv_w', 'L0_attn_Wv_b', 'L0_attn_Wo_w', 'L0_attn_Wo_b',
        'L0_ffn_W_gate', 'L0_ffn_b_gate', 'L0_ffn_W_e', 'L0_ffn_b_e']
_OUTS = [((B, N, D), 'float32')]


def kernel(**inputs):
    import numpy as _np
    import concourse.bacc as _bacc
    from concourse import mybir as _mybir
    from concourse.bass_utils import run_bass_kernel_spmd as _run

    nc = _bacc.Bacc("TRN2", target_bir_lowering=False, num_devices=1)
    arrays, args = {}, []
    for name in _INS:
        a = _np.ascontiguousarray(inputs[name])
        arrays[f"in_{name}_dram"] = a
        args.append(nc.dram_tensor(f"in_{name}_dram", a.shape, _mybir.dt.from_np(a.dtype), kind="ExternalInput").ap())
    for i, (shape, dtype) in enumerate(_OUTS):
        dt = _mybir.dt.from_np(_np.dtype(dtype))
        args.append(nc.dram_tensor(f"out_{i}_dram", shape, dt, kind="ExternalOutput").ap())
    attention_and_experts(nc, *args)
    r = _run(nc, [arrays], core_ids=[0])
    return r.results[0]["out_0_dram"]
```
